# Optimizing a Trainium2 kernel written in Bass

```python
import numpy as np
import jax
import jax.numpy as jnp

def _softmax(x, axis=-1):
    return jax.nn.softmax(x, axis=axis)

def _gelu(x):
    return jax.nn.gelu(x, approximate=True)

def _silu(x):
    return jax.nn.silu(x)

def _sigmoid(x):
    return jax.nn.sigmoid(x)

def _layernorm(x, axis=-1, eps=1e-05):
    m = jnp.mean(x, axis=axis, keepdims=True)
    v = jnp.var(x, axis=axis, keepdims=True)
    return (x - m) / jnp.sqrt(v + eps)

def _scatter_add(tgt, idx, src, axis=0):
    return tgt.at[idx].add(src)

def _segment_sum(src, seg, n):
    return jax.ops.segment_sum(src, seg, n)
kernel_name = 'mk_hybrid_d1_jaxref_r8_02cb15'

def setup_inputs(seed: int=0):
    np.random.seed(seed)
    _w = jnp.asarray

    def _L0_attn_a_setup():
        import jax, jax.numpy as jnp
        import numpy as np
        E = 256
        H = 16
        D = E // H
        B = 4
        N = 256
        key = jax.random.key(seed)
        ks = jax.random.split(key, 5)
        scale_qkv = 1.0 / np.sqrt(E)
        scale_fc = 1.0 / np.sqrt(E)
        return {'x': jax.random.normal(ks[0], (B, N, E), dtype=jnp.float32), 'w_qkv': jax.random.uniform(ks[1], (E, E + 2 * D), jnp.float32, -scale_qkv, scale_qkv), 'b_qkv': jax.random.uniform(ks[2], (E + 2 * D,), jnp.float32, -scale_qkv, scale_qkv), 'w_fc': jax.random.uniform(ks[3], (E, E), jnp.float32, -scale_fc, scale_fc), 'b_fc': jax.random.uniform(ks[4], (E,), jnp.float32, -scale_fc, scale_fc)}
    _L0_attn_a_in = _L0_attn_a_setup()

    def _L0_attn_b_setup():
        import jax, jax.numpy as jnp
        import numpy as np
        D_MODEL = 256
        N_HEADS = 16
        HEAD_DIM = D_MODEL // N_HEADS
        B, T = (2, 256)

        def _alibi_bias(n_heads: int, seq_len: int) -> jnp.ndarray:
            exponents = jnp.arange(1, n_heads + 1, dtype=jnp.float32)
            slopes = 0.5 ** (exponents * 8.0 / n_heads)
            pos = jnp.arange(seq_len, dtype=jnp.float32)
            rel = pos[None, :] - pos[:, None]
            bias = slopes[:, None, None] * rel[None]
            causal = pos[None, :] <= pos[:, None]
            return jnp.where(causal[None], bias, -jnp.inf)
        key = jax.random.key(seed)
        ks = jax.random.split(key, 5)
        s = 1.0 / np.sqrt(D_MODEL)
        x = jax.random.normal(ks[0], (B, T, D_MODEL), dtype=jnp.float32)
        Wq = jax.random.uniform(ks[1], (D_MODEL, D_MODEL), jnp.float32, -s, s)
        Wk = jax.random.uniform(ks[2], (D_MODEL, D_MODEL), jnp.float32, -s, s)
        Wv = jax.random.uniform(ks[3], (D_MODEL, D_MODEL), jnp.float32, -s, s)
        Wo = jax.random.uniform(ks[4], (D_MODEL, D_MODEL), jnp.float32, -s, s)
        return {'x': x, 'Wq': Wq, 'Wk': Wk, 'Wv': Wv, 'Wo': Wo}
    _L0_attn_b_in = _L0_attn_b_setup()

    def _L0_ffn_setup():
        import jax, jax.numpy as jnp
        import numpy as np
        B, S, D = (2, 256, 256)
        E = 8
        TOPK = 2
        H_SHARED = 1024
        H_ROUTED = 128
        STD = 0.02
        key = jax.random.key(seed)
        ks = jax.random.split(key, 7)
        return {'x': jax.random.normal(ks[0], (B, S, D), jnp.float32), 'w12': jax.random.normal(ks[1], (E, 2 * H_ROUTED, D), jnp.float32) * STD, 'w3': jax.random.normal(ks[2], (E, D, H_ROUTED), jnp.float32) * STD, 'router_w': jax.random.normal(ks[3], (E, D), jnp.float32) * STD, 'expert_bias': jnp.zeros((E,), jnp.float32), 'sw1': jax.random.normal(ks[4], (H_SHARED, D), jnp.float32) * STD, 'sw2': jax.random.normal(ks[5], (H_SHARED, D), jnp.float32) * STD, 'sw3': jax.random.normal(ks[6], (D, H_SHARED), jnp.float32) * STD}
    _L0_ffn_in = _L0_ffn_setup()
    _d = {'L0_attn_a_x': _L0_attn_a_in['x'], 'L0_attn_a_w_qkv': _L0_attn_a_in['w_qkv'], 'L0_attn_a_b_qkv': _L0_attn_a_in['b_qkv'], 'L0_attn_a_w_fc': _L0_attn_a_in['w_fc'], 'L0_attn_a_b_fc': _L0_attn_a_in['b_fc'], 'L0_attn_b_Wq': _L0_attn_b_in['Wq'], 'L0_attn_b_Wk': _L0_attn_b_in['Wk'], 'L0_attn_b_Wv': _L0_attn_b_in['Wv'], 'L0_attn_b_Wo': _L0_attn_b_in['Wo'], 'L0_ffn_w12': _L0_ffn_in['w12'], 'L0_ffn_w3': _L0_ffn_in['w3'], 'L0_ffn_router_w': _L0_ffn_in['router_w'], 'L0_ffn_expert_bias': _L0_ffn_in['expert_bias'], 'L0_ffn_sw1': _L0_ffn_in['sw1'], 'L0_ffn_sw2': _L0_ffn_in['sw2'], 'L0_ffn_sw3': _L0_ffn_in['sw3']}
    _x0 = _d['L0_attn_a_x']
    _d['L0_attn_a_x'] = jax.random.normal(jax.random.fold_in(jax.random.key(seed), 1), (2, 1024, 256), dtype=_x0.dtype)
    del _x0
    return _d

def reference(L0_attn_a_x, L0_attn_a_w_qkv, L0_attn_a_b_qkv, L0_attn_a_w_fc, L0_attn_a_b_fc, L0_attn_b_Wq, L0_attn_b_Wk, L0_attn_b_Wv, L0_attn_b_Wo, L0_ffn_w12, L0_ffn_w3, L0_ffn_router_w, L0_ffn_expert_bias, L0_ffn_sw1, L0_ffn_sw2, L0_ffn_sw3):

    def _L0_attn_a_ref(x, w_qkv, b_qkv, w_fc, b_fc):
        import jax, jax.numpy as jnp
        import numpy as np
        E = 256
        H = 16
        D = E // H
        B = 4
        N = 256
        b, n, _ = x.shape
        qkv = x @ w_qkv + b_qkv
        q = qkv[..., :E].reshape(b, n, H, D)
        k = qkv[..., E:E + D]
        v = qkv[..., E + D:]
        scores = jnp.einsum('bnhd,bmd->bhnm', q, k) / jnp.sqrt(jnp.float32(D))
        causal = jnp.triu(jnp.ones((n, n), dtype=bool), k=1)
        scores = jnp.where(causal, -jnp.inf, scores)
        attn = jax.nn.softmax(scores, axis=-1)
        out = jnp.einsum('bhnm,bmd->bnhd', attn, v)
        out = out.reshape(b, n, E)
        return out @ w_fc + b_fc

    def _L0_attn_b_ref(x, Wq, Wk, Wv, Wo):
        import jax, jax.numpy as jnp
        import numpy as np
        D_MODEL = 256
        N_HEADS = 16
        HEAD_DIM = D_MODEL // N_HEADS
        B, T = (2, 256)

        def _alibi_bias(n_heads: int, seq_len: int) -> jnp.ndarray:
            exponents = jnp.arange(1, n_heads + 1, dtype=jnp.float32)
            slopes = 0.5 ** (exponents * 8.0 / n_heads)
            pos = jnp.arange(seq_len, dtype=jnp.float32)
            rel = pos[None, :] - pos[:, None]
            bias = slopes[:, None, None] * rel[None]
            causal = pos[None, :] <= pos[:, None]
            return jnp.where(causal[None], bias, -jnp.inf)
        Bsz, Tlen, _ = x.shape
        H, D = (N_HEADS, HEAD_DIM)

        def split_heads(t):
            return t.reshape(Bsz, Tlen, H, D).transpose(0, 2, 1, 3)
        q = split_heads(x @ Wq.T)
        k = split_heads(x @ Wk.T)
        v = split_heads(x @ Wv.T)
        scale = jnp.sqrt(jnp.float32(D))
        scores = jnp.einsum('bhqd,bhkd->bhqk', q, k) / scale
        scores = scores + _alibi_bias(H, Tlen)[None]
        attn = jax.nn.softmax(scores, axis=-1)
        out = jnp.einsum('bhqk,bhkd->bhqd', attn, v)
        out = out.transpose(0, 2, 1, 3).reshape(Bsz, Tlen, H * D)
        return out @ Wo.T

    def _L0_ffn_ref(x, w12, w3, router_w, expert_bias, sw1, sw2, sw3):
        import jax, jax.numpy as jnp
        import numpy as np
        B, S, D = (2, 256, 256)
        E = 8
        TOPK = 2
        H_SHARED = 1024
        H_ROUTED = 128
        STD = 0.02
        b, s, d = x.shape
        g = x @ sw1.T
        u = x @ sw2.T
        shared_out = jax.nn.silu(g) * u @ sw3.T
        scores = jax.nn.sigmoid(x @ router_w.T)
        selection_scores = scores + expert_bias
        _, top_idx = jax.lax.top_k(selection_scores, TOPK)
        top_scores = jnp.take_along_axis(scores, top_idx, axis=-1)
        top_scores = top_scores / (top_scores.sum(-1, keepdims=True) + 1e-09)
        flat_x = x.reshape(-1, d)
        T = flat_x.shape[0]
        flat_idx = top_idx.reshape(T, TOPK)
        flat_sc = top_scores.reshape(T, TOPK)
        combine = jnp.zeros((T, E), x.dtype).at[jnp.arange(T)[:, None], flat_idx].add(flat_sc)
        h12 = jnp.einsum('td,ehd->teh', flat_x, w12)
        h1, h2 = jnp.split(h12, 2, axis=-1)
        h = jax.nn.silu(h1) * h2
        out_e = jnp.einsum('teh,edh->ted', h, w3)
        routed_out = jnp.einsum('ted,te->td', out_e, combine).reshape(b, s, d)
        return shared_out + routed_out
    x = L0_attn_a_x
    x = x + _L0_attn_a_ref(_layernorm(x, axis=-1), L0_attn_a_w_qkv, L0_attn_a_b_qkv, L0_attn_a_w_fc, L0_attn_a_b_fc)
    x = x + _L0_ffn_ref(_layernorm(x, axis=-1), L0_ffn_w12, L0_ffn_w3, L0_ffn_router_w, L0_ffn_expert_bias, L0_ffn_sw1, L0_ffn_sw2, L0_ffn_sw3)
    x = x + _L0_attn_b_ref(_layernorm(x, axis=-1), L0_attn_b_Wq, L0_attn_b_Wk, L0_attn_b_Wv, L0_attn_b_Wo)
    x = x + _L0_ffn_ref(_layernorm(x, axis=-1), L0_ffn_w12, L0_ffn_w3, L0_ffn_router_w, L0_ffn_expert_bias, L0_ffn_sw1, L0_ffn_sw2, L0_ffn_sw3)
    return x

_drawn_inputs = setup_inputs


def setup_inputs(seed=0):
    import zlib

    import numpy as np

    out = dict(_drawn_inputs(seed))
    spreads = {'L0_ffn_expert_bias': (0.0, 0.392)}
    factors = {'L0_ffn_w12': 3.013, 'L0_ffn_w3': 2.742, 'L0_ffn_router_w': 4.367}
    for name, (base, spread) in spreads.items():
        noise = np.random.default_rng([zlib.crc32(name.encode()), seed]).standard_normal(out[name].shape)
        drawn = base * np.exp(spread * noise) if base else spread * noise
        out[name] = jnp.asarray(drawn.astype(out[name].dtype))
    for name, factor in factors.items():
        out[name] = (out[name] * factor).astype(out[name].dtype)
    return out
```

```python
from contextlib import ExitStack

import numpy as np

import concourse.bass as bass
from concourse import mybir

F32 = mybir.dt.float32
F32R = mybir.dt.float32r
BF16 = mybir.dt.bfloat16
U16 = mybir.dt.uint16
U32 = mybir.dt.uint32
ACT = mybir.ActivationFunctionType
ALU = mybir.AluOpType
AX = mybir.AxisListType

NB, N, E = 2, 1024, 256
H, D = 16, 16
P = 128
T = NB * N
TT = T // P
CH = 512
NCH = T // CH
TC = CH // P
KE = E // P
G = H // 4
STEPS = NB * G
QT = N // P
HALF = QT // 2
NEXP = 8
UNITS = 16
FS = UNITS * NCH
EPS = 1e-5
NEG = -1e30
ROWS = 96
ALIBI = 6
PRODUCTS = [(0, 0), (1, 0), (2, 0), (0, 1), (1, 1), (0, 2)]
SBANKS = 3


def score_units():
    units = []
    for qt in range(QT):
        if qt >= HALF:
            units += [(qt, 0, j, 1, CH, False) for j in range(4)]
        width = P * (qt % HALF + 1)
        share = min(4, CH // width)
        units += [(qt, qt // HALF, j, share, width, True) for j in range(0, 4, share)]
    return units


SU = score_units()
NSU = len(SU) + 1


def units_by_slot(share):
    work = [N - P * (n // 4) + P for n in range(4 * QT)]
    bound = [min(len(SU), round(len(SU) * sum(work[:n + 1]) / (share * sum(work)))) for n in range(4 * QT)]
    return list(zip([0] + bound, bound))


UNITS_BEHIND = units_by_slot(0.85)
MAXIMA_BEHIND = next(n for n, (_, end) in enumerate(UNITS_BEHIND) if end == len(SU)) + 2
PV_BEHIND = (1, 3)
INVERT_AT, DIVIDE_AT = 12, 28
QKV = [[("kv", 0), ("q", 0), ("q", 1)],
       [("q", 0), ("q", 1), ("k", 0), ("k", 1), ("v", 0), ("v", 1)]]
SPLIT = [3, 4]


def qkv_index(l, c, m):
    return (l and NCH * len(QKV[0])) + len(QKV[l]) * c + m


def split_index(l, c, m):
    return (l and NCH * SPLIT[0]) + SPLIT[l] * c + m


def turns(l, s):
    return (l and len(range(s % SBANKS, STEPS, SBANKS))), s // SBANKS + 1


def wait(eng, sem, count):
    if not isinstance(count, int) or count > 0:
        eng.wait_ge(sem, count)


def split_product(pe, out, terms):
    for n, (lh, ll, rh, rl) in enumerate(terms):
        pe.matmul(out, lh, rh, start=n == 0, stop=False)
        pe.matmul(out, ll, rh, start=False, stop=False)
        last = pe.matmul(out, lh, rl, start=False, stop=n == len(terms) - 1)
    return last


def program(nc, x, w_a, b_a, fc_a, w_b, fc_b, w_units, router, ebias, iota, consts, slopes, krows, out):
    x_v = x.rearrange("b (t p) e -> p (b t) e", p=P)
    out_v = out.rearrange("b (t p) e -> p (b t) e", p=P)
    w_a_v = w_a.rearrange("(k p) m -> p k m", p=P)
    w_b_v = w_b.rearrange("(k p) m -> p k m", p=P)
    router_v = router.rearrange("(k p) m -> p k m", p=P)
    q_parts = [nc.dram_tensor(f"q_parts{l}", (3, E, T), BF16).ap() for l in range(2)]
    inverses = nc.dram_tensor("inverses", (2 * STEPS, 4, N), F32).ap()
    k_parts = [nc.dram_tensor(f"k_parts{l}", (3, (D, E)[l], T), BF16).ap() for l in range(2)]

    with ExitStack() as ctx:
        def sb(name, shape, dt):
            return ctx.enter_context(nc.sbuf_tensor(name, shape, dt))

        def sem(name):
            return ctx.enter_context(nc.semaphore(name))

        xs = sb("xs", [P, TT, E], F32)
        st = sb("st", [P, TT, 6], F32)
        mv = sb("mv", [P, TT, 2], F32)
        ve = sb("ve", [P, TT], F32)
        rstd = sb("rstd", [P, TT], F32)
        zero = sb("zero", [P, 1], F32)
        mhalf = sb("mhalf", [P, TC], F32)
        cst = sb("cst", [P, 3, P], F32)
        ident = cst[:, 0, :]
        cstb = sb("cstb", [P, 3, P], BF16)
        identb, mask_q, mask_k = cstb[:, 0, :], cstb[:, 1, :], cstb[:, 2, :]
        bias_a = sb("bias_a", [P, 3], F32)
        wraw = sb("wraw", [P, KE, 768], F32)
        wp_h, wp_l = (sb(f"wp_{n}", [P, KE, 768], F32R) for n in "hl")
        wfc = sb("wfc", [P, G, E], F32)
        rt_h, rt_l = (sb(f"rt_{n}", [P, KE, P], F32R) for n in "hl")
        vp = sb("vp", [P, TT, H, 32], F32)
        ebb = sb("ebb", [P, NEXP], F32)
        iota8 = sb("iota8", [P, NEXP], F32)
        comb = sb("comb", [P, TT, UNITS], F32)
        mc = sb("mc", [P, 2, 4, QT], F32)
        mab = sb("mab", [P, 2, 2, 4, HALF], F32)
        nmx = sb("nmx", [32, 2, 3, P], BF16)
        nmr = sb("nmr", [32, 2, P], F32)
        sums = sb("sums", [32, 2, P], F32)

        kb = 1024
        size = [32 * kb, 32 * kb, 48 * kb, 8 * kb]
        base = [((nc.sbuf_base + 63) // 64) * 64]
        for n in size:
            base.append(base[-1] + n)
        ctx.enter_context(nc.sbuf_tensor("arena", [P, base[-1] - nc.sbuf_base], mybir.dt.uint8))

        def region(r, plan):
            at, found = base[r], []
            for name, shape, dt in plan:
                found.append(nc.alloc_sbuf_tensor_at(name, shape, dt, offset=at))
                at += int(np.prod(shape[1:])) * (2 if dt == BF16 else 4)
            assert at <= base[r] + size[r], (name, at - base[r])
            return found

        (pt,) = region(0, [("pt", [P, 2, 4, N], F32)])
        xt_h, xt_l = region(0, [(f"xt_{n}", [P, KE, T], F32R) for n in "hl"])
        (ot,) = region(1, [("ot", [P, G, T], F32)])
        yb, yr, hml, sg8, sc, sel, eq0, eq1, top, idx, idf, ssum = region(1, [
            ("yb", [P, 2, CH], F32), ("yr", [P, 2, CH], F32), ("hml", [P, 2, 3, CH], BF16),
            ("sg8", [NEXP, NCH, CH], F32), ("sc", [P, TT, NEXP], F32), ("sel", [P, TT, NEXP], F32),
            ("eq0", [P, TT, NEXP], F32), ("eq1", [P, TT, NEXP], F32), ("top", [P, TT, 8], F32),
            ("idx", [P, TT, 8], U32), ("idf", [P, TT, 2], F32), ("ssum", [P, 2, TT], F32)])
        qs, ks = region(2, [(f"{n}s", [P, SBANKS, 4, N], BF16) for n in "qk"])
        wr, = region(2, [("wr", [P, 2, 768], F32)])
        wu_h, wu_l = (nc.alloc_sbuf_tensor_at(f"wu_{n}", [P, 2, 768], F32R, offset=base[2] + (6 + 6 * m) * kb)
                      for m, n in enumerate("hl"))
        hf, sg = (nc.alloc_sbuf_tensor_at(n, [P, 2, CH], F32, offset=base[2] + (18 + 4 * m) * kb)
                  for m, n in enumerate(("hf", "sg")))
        hh, hl = (nc.alloc_sbuf_tensor_at(n, [P, 2, CH], F32R, offset=base[2] + (26 + 4 * m) * kb)
                  for m, n in enumerate(("hh", "hl")))

        (xn,) = region(3, [("xn", [P, 2, TC, E], F32)])
        ou, inv = region(3, [("ou", [P, N], F32), ("inv", [P, N], F32)])

        st_ps = [ctx.enter_context(nc.psum_tensor(f"st_ps{n}", [P, N], F32)) for n in range(2)]
        o_ps = ctx.enter_context(nc.psum_tensor("o_ps", [P, N], F32))
        su_ps = [ctx.enter_context(nc.psum_tensor(f"su_ps{n}", [P, CH], F32)) for n in range(2)]
        bank = [st_ps[0][:, 0:CH], st_ps[0][:, CH:N], st_ps[1][:, 0:CH], st_ps[1][:, CH:N],
                o_ps[:, 0:CH], o_ps[:, CH:N], su_ps[0][:, :], su_ps[1][:, :]]

        x_in = [sem(f"x_in{c}") for c in range(NCH)]
        const_in, wraw_in, wfc_in, unit_in = sem("const_in"), sem("wraw_in"), sem("wfc_in"), [sem("unit_in0"), sem("unit_in1")]
        const_ready, w_split, unit_split, ones_set = sem("const_ready"), sem("w_split"), sem("unit_split"), sem("ones_set")
        ln_stats, ln_aggr, ln_var, ln_rstd, xn_done = (sem(n) for n in ("ln_stats", "ln_aggr", "ln_var", "ln_rstd", "xn_done"))
        tr_done, xth_done, xtl_done = sem("tr_done"), sem("xth_done"), sem("xtl_done")
        qkv_done, evac_done, vt_done, vc_done = sem("qkv_done"), sem("evac_done"), sem("vt_done"), sem("vc_done")
        part_step, parts_done, parts_out = sem("part_step"), sem("parts_done"), [sem("parts_out0"), sem("parts_out1")]
        stk_in = [sem(f"stk_in{n}") for n in range(SBANKS)]
        max_in = [sem(f"max_in{n}") for n in range(SBANKS)]
        keys_in = sem("keys_in")
        su_ready, su_used, mc_done, nm_step, nm_done = (sem(n) for n in ("su_ready", "su_used", "mc_done", "nm_step", "nm_done"))
        st_ready, p_ready, pv_done, ou_done, inv_done, ot_done = (
            sem(n) for n in ("st_ready", "p_ready", "pv_done", "ou_done", "inv_done", "ot_done"))
        sums_in, inv_out, inv_in = sem("sums_in"), sem("inv_out"), sem("inv_in")
        fc_done, fc_added = sem("fc_done"), sem("fc_added")
        rt_done, sig_done, rtt_done, rt_used, rt_step, comb_done = (
            sem(n) for n in ("rt_done", "sig_done", "rtt_done", "rt_used", "rt_step", "comb_done"))
        g_ready, u_ready, silu_done, h_done, hh_done, hl_done, down_done, added = (
            sem(n) for n in ("g_ready", "u_ready", "silu_done", "h_done", "hh_done", "hl_done", "down_done", "added"))
        out_sent = sem("out_sent")

        def step_no(l, s):
            return STEPS * l + s

        def stk_count(l, s):
            before, own = turns(l, s)
            return 16 * (len(PRODUCTS) * before + (len(PRODUCTS), 2 * len(PRODUCTS) + 1)[l] * own)

        def max_count(l, s):
            before, own = turns(l, s)
            return 16 * 3 * (before + own)

        def batch_parts_out(l, b):
            return 16 * split_index(l, NCH // NB * (b + 1), 0) // 2

        block = ctx.enter_context(nc.Block())

        @block.sync
        def _(sp):
            for c in range(NCH):
                sp.dma_start(xs[:, TC * c:TC * c + TC, :], x_v[:, TC * c:TC * c + TC, :]).then_inc(x_in[c], 16)
                if c == 0:
                    sp.dma_start(cst[:, :, :], consts).then_inc(const_in, 16)
                    sp.dma_start(wraw[:, :, 0:3 * P], w_a_v).then_inc(wraw_in, 16)
            sp.dma_start(bias_a[:, :], b_a).then_inc(const_in, 16)
            sp.dma_start(ebb[:, :], ebias.partition_broadcast(P)).then_inc(const_in, 16)
            sp.dma_start(iota8[:, :], iota).then_inc(const_in, 16)
            sp.dma_start(wfc[:, :, :], fc_a).then_inc(wfc_in, 16)
            sp.wait_ge(w_split, 2)
            sp.dma_start(wraw[:, :, 0:P], router_v).then_inc(wraw_in, 16)
            sp.wait_ge(w_split, 4)
            sp.dma_start(wraw[:, :, :], w_b_v).then_inc(wraw_in, 16)

            def send_parts(l, c):
                for m in range(SPLIT[l]):
                    kind, mt = QKV[l][m]
                    n = split_index(l, c, m)
                    sp.wait_ge(parts_done, n + 1)
                    if kind == "kv":
                        dst, src = k_parts[l][:, :, CH * c:CH * c + CH], hml[0:D, n % 2, :, :]
                    else:
                        dst = (k_parts if kind == "k" else q_parts)[l][:, P * mt:P * mt + P, CH * c:CH * c + CH]
                        src = hml[:, n % 2, :, :]
                    sp.dma_start(dst.rearrange("t p n -> p t n"), src).then_inc(parts_out[n % 2], 16)

            def load_stack(l, s):
                b, g = divmod(s, G)
                r = s % SBANKS
                if s >= SBANKS:
                    sp.wait_ge(st_ready, 4 * QT * (step_no(l, s - SBANKS) + 1))
                for i, pq in enumerate(PRODUCTS):
                    for stack, parts, part in ((qs, q_parts, pq[0]), (ks, k_parts, pq[1]))[:1 + l]:
                        src = parts[l][part, 4 * D * g:4 * D * (g + 1), N * b:N * b + N]
                        sp.dma_start(stack[D * i:D * i + D, r, :, :],
                                     src.rearrange("(j d) n -> d j n", d=D)).then_inc(stk_in[r], 16)
                if l:
                    sp.dma_start(qs[ROWS:ROWS + ALIBI, r, :, :].bitcast(U16),
                                 slopes[:, 4 * g:4 * g + 4, :]).then_inc(stk_in[r], 16)

            def load_keys(l, b):
                if l == 0:
                    for i, (_, pk) in enumerate(PRODUCTS):
                        sp.dma_start(ks[D * i:D * i + D, b, 0, :], k_parts[0][pk, :, N * b:N * b + N]).then_inc(keys_in, 16)
                    sp.dma_start(ks[ROWS:ROWS + 3, b, 0, :].bitcast(U16), krows[ALIBI:, :]).then_inc(keys_in, 16)
                elif b == 0:
                    for r in range(SBANKS):
                        for j in range(4):
                            sp.dma_start(ks[ROWS:ROWS + ALIBI + 3, r, j, :].bitcast(U16), krows).then_inc(keys_in, 16)

            def send_maxima(l, s):
                r, S = s % SBANKS, step_no(l, s)
                sp.wait_ge(nm_done, S + 1)
                for part in range(3):
                    row = ROWS + l * ALIBI + part
                    sp.dma_start(qs[row:row + 1, r, :, :], nmx[:, S % 2, part, :]).then_inc(max_in[r], 16)

            def gather_sums(S):
                sp.wait_ge(ou_done, S + 1)
                sp.dma_start(sums[:, 0, :], ou[D:P:32, :]).then_inc(sums_in, 16)

            def spread_inverses(S):
                sp.wait_ge(inv_done, S + 1)
                sp.dma_start(inverses[S], sums[:, 1, :]).then_inc(inv_out, 16)
                sp.wait_ge(inv_out, 16 * (S + 1))
                for j in range(4):
                    sp.dma_start(inv[32 * j:32 * j + 32, :], inverses[S, j].partition_broadcast(32)).then_inc(inv_in, 16)

            def attention(l):
                for b in range(NB):
                    for c in range(NCH // NB * b, NCH // NB * (b + 1)):
                        send_parts(l, c)
                    for n in range(2):
                        sp.wait_ge(parts_out[n], batch_parts_out(l, b))
                    load_keys(l, b)
                    if b == 0:
                        for s in range(SBANKS):
                            load_stack(l, s)
                for s in range(STEPS):
                    send_maxima(l, s)
                    if s:
                        gather_sums(step_no(l, s - 1))
                    if s >= 1 and s + 2 < STEPS:
                        load_stack(l, s + 2)
                    if s:
                        spread_inverses(step_no(l, s - 1))
                gather_sums(step_no(l, STEPS - 1))
                spread_inverses(step_no(l, STEPS - 1))
                if l == 0:
                    sp.wait_ge(fc_done, QT)
                    sp.dma_start(wfc[:, :, :], fc_b).then_inc(wfc_in, 16)

            def experts(f):
                sp.wait_ge(st_ready, 4 * QT * STEPS * (f + 1))
                for u in range(2):
                    sp.dma_start(wr[:, u, :], w_units[u]).then_inc(unit_in[u], 16)
                with sp.Fori(1, UNITS // 2) as i:
                    for u in range(2):
                        sp.wait_ge(unit_split, 2 * (UNITS * f) + 4 * i + 2 * u - 2)
                        sp.dma_start(wr[:, u, :], w_units[2 * i + u]).then_inc(unit_in[u], 16)

            attention(0)
            experts(0)
            attention(1)
            experts(1)
            for c in range(NCH):
                sp.wait_ge(added, TC * (2 * FS - NCH + c + 1))
                sp.dma_start(out_v[:, TC * c:TC * c + TC, :], xs[:, TC * c:TC * c + TC, :]).then_inc(out_sent, 16)
            sp.wait_ge(out_sent, 16 * NCH)

        @block.gpsimd
        def _(pool):
            pool.memset(mhalf[:, :], -0.5).then_inc(ones_set, 1)
            pool.memset(zero[:, :], 0.0).then_inc(ones_set, 1)
            pool.memset(vp[:, :, :, :], 1.0).then_inc(ones_set, 1)
            pool.memset(comb[:, :, :], 1.0).then_inc(ones_set, 1)

            def rstds(p):
                for c in range(NCH):
                    t = slice(TC * c, TC * c + TC)
                    pool.wait_ge(ln_aggr, TT * p + TC * (c + 1))
                    pool.tensor_scalar(ve[:, t], mv[:, t, 1], EPS, None, ALU.add).then_inc(ln_var, 1)
                    pool.wait_ge(ln_var, NCH * p + c + 1)
                    pool.tensor_tensor(rstd[:, t], ve[:, t], mhalf[:, :], ALU.pow).then_inc(ln_rstd, 1)

            def split_weights(n, hi, lo, m):
                pool.wait_ge(wraw_in, 16 * (n + 1))
                pool.tensor_copy(hi, wraw[:, :, 0:m]).then_inc(w_split, 1)
                pool.wait_ge(w_split, 2 * n + 1)
                pool.tensor_tensor(lo, wraw[:, :, 0:m], hi.bitcast(F32), ALU.subtract).then_inc(w_split, 1)

            def split_unit(f, u, i):
                n = UNITS * f + 2 * i + u
                pool.wait_ge(unit_in[u], 16 * (UNITS // 2 * f + i + 1))
                if not isinstance(i, int):
                    pool.wait_ge(down_done, 4 * n - 4)
                pool.tensor_tensor(wu_h[:, u, :], wr[:, u, :], zero[:, :].to_broadcast([P, 768]), ALU.subtract).then_inc(unit_split, 1)
                pool.wait_ge(unit_split, 2 * n + 1)
                pool.tensor_tensor(wu_l[:, u, :], wr[:, u, :], wu_h[:, u, :].bitcast(F32), ALU.subtract).then_inc(unit_split, 1)

            def experts(f):
                for u in range(2):
                    split_unit(f, u, 0)
                with pool.Fori(1, UNITS // 2) as i:
                    for u in range(2):
                        split_unit(f, u, i)

            pool.wait_ge(ones_set, 4)
            split_weights(0, wp_h[:, :, 0:3 * P], wp_l[:, :, 0:3 * P], 3 * P)
            rstds(0)
            split_weights(1, rt_h[:, :, :], rt_l[:, :, :], P)
            pool.wait_ge(qkv_done, NCH * len(QKV[0]))
            split_weights(2, wp_h[:, :, :], wp_l[:, :, :], 768)
            rstds(1)
            experts(0)
            rstds(2)
            rstds(3)
            experts(1)

        @block.tensor
        def _(pe):
            def ln_transposes(p):
                for c in range(NCH):
                    pe.wait_ge(xn_done, TT * p + TC * (c + 1))
                    for k in range(KE):
                        n = KE * (NCH * p + c) + k
                        wait(pe, xtl_done, n - 3)
                        for t in range(TC):
                            last = pe.transpose(bank[n % 4][:, P * t:P * t + P], xn[:, c % 2, t, P * k:P * k + P], ident)
                        last.then_inc(tr_done, 1)

            def qkv(l):
                pe.wait_ge(w_split, 2 + 4 * l)
                if l:
                    pe.wait_ge(added, TC * FS)
                for c in range(NCH):
                    pe.wait_ge(xtl_done, KE * (NCH * 2 * l + c + 1))
                    tok = slice(CH * c, CH * c + CH)
                    for m, (kind, mt) in enumerate(QKV[l]):
                        n = qkv_index(l, c, m)
                        out_b = bank[4 + n % 4]
                        wait(pe, evac_done, n - 3)
                        if l == 0 and (n - 4) >= 0 and (n - 4) % 3 == 0:
                            pe.wait_ge(vc_done, (n - 4) // 3 + 1)
                        if kind == "v":
                            for t in range(2):
                                tt = TC * c + 2 * mt + t
                                ts = slice(P * tt, P * tt + P)
                                last = split_product(pe, out_b[:, E * t:E * t + E], [
                                    (xt_h[:, k, ts], xt_l[:, k, ts], wp_h[:, k, 2 * E:], wp_l[:, k, 2 * E:]) for k in range(KE)])
                        else:
                            col = P * (m if l == 0 else {"q": 0, "k": 2}[kind] + mt)
                            last = split_product(pe, out_b, [
                                (wp_h[:, k, col:col + P], wp_l[:, k, col:col + P], xt_h[:, k, tok], xt_l[:, k, tok])
                                for k in range(KE)])
                        last.then_inc(qkv_done, 1)
                    if l == 0:
                        n = qkv_index(l, c, 0)
                        pe.wait_ge(evac_done, n + 1)
                        for t in range(TC):
                            last = pe.transpose(bank[4 + n % 4][:, 32 * t:32 * t + 32],
                                                yb[0:32, split_index(l, c, 0) % 2, P * t:P * t + P], ident[0:32, 0:32])
                        last.then_inc(vt_done, 1)

            def key_stack(l, s):
                return (lambda j: ks[:, s // G, 0, :]) if l == 0 else (lambda j: ks[:, s % SBANKS, j, :])

            def query_major(l, s, u):
                qt, half, j0, share, width, diagonal = SU[u]
                n = NSU * step_no(l, s) + u
                if u == 0:
                    pe.wait_ge(stk_in[s % SBANKS], stk_count(l, s))
                out_b = bank[6 + n % 2]
                wait(pe, su_used, n - 1)
                rows = ROWS + l * ALIBI
                for a in range(share):
                    c0 = a * width
                    last = pe.matmul(out_b[:, c0:c0 + width], qs[0:rows, s % SBANKS, j0 + a, P * qt:P * qt + P],
                                     key_stack(l, s)(j0 + a)[0:rows, CH * half:CH * half + width],
                                     start=True, stop=not diagonal)
                    if diagonal:
                        last = pe.matmul(out_b[:, c0 + width - P:c0 + width], identb, mask_q, start=False, stop=True)
                last.then_inc(su_ready, 1)

            def transpose_maxima(l, s):
                S = step_no(l, s)
                n = NSU * S + NSU - 1
                pe.wait_ge(mc_done, S + 1)
                pe.wait_ge(su_used, n - 1)
                pe.transpose(bank[6 + n % 2][0:32, 0:P], mc[:, S % 2, :, :].rearrange("p j t -> p (j t)"), ident).then_inc(su_ready, 1)

            def key_major(l, s, kt, j):
                n = 4 * QT * step_no(l, s) + 4 * kt + j
                if kt == 0 and j == 0:
                    pe.wait_ge(max_in[s % SBANKS], max_count(l, s))
                wait(pe, p_ready, n - 1)
                rows = ROWS + l * ALIBI + 3
                first = P * kt
                for lo, hi in ([(first, CH), (CH, N)] if kt < HALF else [(first, N)]):
                    diagonal = lo == first
                    last = pe.matmul(st_ps[n % 2][:, lo:hi], key_stack(l, s)(j)[0:rows, first:first + P],
                                     qs[0:rows, s % SBANKS, j, lo:hi], start=True, stop=not diagonal)
                    if diagonal:
                        last = pe.matmul(st_ps[n % 2][:, lo:lo + P], identb, mask_k, start=False, stop=True)
                last.then_inc(st_ready, 1)

            def values(l, s, kt, part):
                S = step_no(l, s)
                b, g = divmod(s, G)
                if kt == 0 and part == 0:
                    wait(pe, ou_done, S)
                if part == 0 or kt >= HALF:
                    pe.wait_ge(p_ready, 4 * QT * S + 4 * kt + 4)
                lo, hi = (P * kt, CH) if part == 0 else (max(CH, P * kt), N)
                for j in range(4):
                    last = pe.matmul(o_ps[32 * j:32 * j + 32, lo:hi], vp[:, QT * b + kt, (4 * g + j) * l, :],
                                     pt[:, kt % 2, j, lo:hi], start=kt == 0,
                                     stop=kt == (HALF - 1 if part == 0 else QT - 1))
                if part == 1:
                    last.then_inc(pv_done, 1)

            def attention(l):
                pe.wait_ge(evac_done, qkv_index(l, NCH - 1, len(QKV[l]) - 1) + 1)
                if l == 0:
                    pe.wait_ge(vc_done, NCH)
                pe.wait_ge(keys_in, 16 * (NB * (len(PRODUCTS) + 1) + l * SBANKS * 4))
                for u in range(NSU - 1):
                    query_major(l, 0, u)
                transpose_maxima(l, 0)
                for s in range(STEPS):
                    for n in range(4 * QT):
                        kt, j = divmod(n, 4)
                        key_major(l, s, kt, j)
                        if kt and j == PV_BEHIND[0] and kt <= HALF:
                            values(l, s, kt - 1, 0)
                        if kt and j == PV_BEHIND[1]:
                            values(l, s, kt - 1, 1)
                        if s + 1 < STEPS:
                            for u in range(*UNITS_BEHIND[n]):
                                query_major(l, s + 1, u)
                            if n == MAXIMA_BEHIND:
                                transpose_maxima(l, s + 1)
                    values(l, s, QT - 1, 1)

            def output_projection(l):
                pe.wait_ge(wfc_in, 16 * (l + 1))
                for q in range(TT // 2):
                    n = TT // 2 * l + q
                    pe.wait_ge(ot_done, STEPS * l + G * (2 * (2 * q) // TT + 1))
                    if q == 2:
                        pe.wait_ge(ou_done, STEPS * (l + 1))
                    if q >= 4:
                        pe.wait_ge(fc_added, n - 3)
                    out_b = bank[(6, 7, 4, 5)[q % 4]]
                    for t in range(2):
                        tt = 2 * q + t
                        for g in range(G):
                            last = pe.matmul(out_b[:, E * t:E * t + E], ot[:, g, P * tt:P * tt + P], wfc[:, g, :],
                                             start=g == 0, stop=g == G - 1)
                    last.then_inc(fc_done, 1)

            def route(f):
                pe.wait_ge(w_split, 4)
                pe.wait_ge(fc_added, TT // 2 * (f + 1))
                for c in range(NCH):
                    pe.wait_ge(xtl_done, KE * (NCH * (2 * f + 1) + c + 1))
                    tok = slice(CH * c, CH * c + CH)
                    split_product(pe, bank[4 + c], [(rt_h[:, k, :], rt_l[:, k, :], xt_h[:, k, tok], xt_l[:, k, tok])
                                                    for k in range(KE)]).then_inc(rt_done, 1)
                for c in range(NCH):
                    pe.wait_ge(sig_done, NCH * f + c + 1)
                    for t in range(TC):
                        last = pe.transpose(bank[4 + c][:, NEXP * t:NEXP * t + NEXP], sg8[:, c, P * t:P * t + P], ident[0:NEXP, 0:NEXP])
                    last.then_inc(rtt_done, 1)

            def up(f, i, e):
                s = FS * f + 8 * i + e
                u, c = divmod(e, NCH)
                tok = slice(CH * c, CH * c + CH)
                if c == 0:
                    pe.wait_ge(unit_split, 2 * (UNITS * f + 2 * i + u + 1))
                wait(pe, h_done, s - 1)
                for a, ready in enumerate((g_ready, u_ready)):
                    split_product(pe, bank[2 * (e % 2) + a], [
                        (wu_h[:, u, E * a + P * k:E * a + P * k + P], wu_l[:, u, E * a + P * k:E * a + P * k + P],
                         xt_h[:, k, tok], xt_l[:, k, tok]) for k in range(KE)]).then_inc(ready, 1)

            def down(f, i, e):
                s = FS * f + 8 * i + e
                u, c = divmod(e, NCH)
                pe.wait_ge(hl_done, s + 1)
                wait(pe, added, TC * (s - 1))
                for t in range(TC):
                    ts = slice(P * t, P * t + P)
                    last = split_product(pe, bank[4 + 2 * (e % 2) + t // 2][:, E * (t % 2):E * (t % 2) + E], [
                        (hh[:, e % 2, ts], hl[:, e % 2, ts], wu_h[:, u, 2 * E:], wu_l[:, u, 2 * E:])])
                last.then_inc(down_done, 1)

            def experts(f):
                for e in range(8):
                    up(f, 0, e)
                    if e == 0:
                        pe.wait_ge(rt_used, NCH * (f + 1))
                    else:
                        down(f, 0, e - 1)
                with pe.Fori(1, UNITS // 2) as i:
                    for e in range(8):
                        up(f, i, e)
                        if e:
                            down(f, i, e - 1)
                        else:
                            down(f, i - 1, 7)
                down(f, UNITS // 2 - 1, 7)

            pe.wait_ge(const_ready, 3)
            pe.wait_ge(ones_set, 4)
            for l in range(2):
                ln_transposes(2 * l)
                qkv(l)
                attention(l)
                output_projection(l)
                ln_transposes(2 * l + 1)
                route(l)
                experts(l)

        @block.scalar
        def _(act):
            def x_hi(p):
                for n in range(KE * NCH * p, KE * NCH * (p + 1)):
                    c, k = divmod(n % (KE * NCH), KE)
                    act.wait_ge(tr_done, n + 1)
                    act.copy(xt_h[:, k, CH * c:CH * c + CH], bank[n % 4]).then_inc(xth_done, 1)

            def qkv(l):
                for c in range(NCH):
                    for m, (kind, mt) in enumerate(QKV[l]):
                        n = qkv_index(l, c, m)
                        act.wait_ge(qkv_done, n + 1)
                        src = bank[4 + n % 4]
                        if kind == "v":
                            tt = TC * c + 2 * mt
                            act.copy(vp[:, tt:tt + 2, :, 0:D], src.rearrange("p (t h d) -> p t h d", t=2, d=D)).then_inc(evac_done, 1)
                            continue
                        y = split_index(l, c, m)
                        wait(act, parts_done, y - 1)
                        if l == 0 and m == 2:
                            act.wait_ge(vt_done, c + 1)
                        if l == 0:
                            act.activation(yb[:, y % 2, :], src, ACT.Identity, bias=bias_a[:, m:m + 1]).then_inc(evac_done, 1)
                        else:
                            act.copy(yb[:, y % 2, :], src).then_inc(evac_done, 1)

            def attention(l):
                for s in range(STEPS):
                    S = step_no(l, s)
                    for n in range(4 * QT):
                        kt, j = divmod(n, 4)
                        i = 4 * QT * S + n
                        act.wait_ge(st_ready, i + 1)
                        wait(act, pv_done, QT * S + kt - 1)
                        act.activation(pt[:, kt % 2, j, P * kt:N], st_ps[i % 2][:, P * kt:N], ACT.Exp,
                                       scale=1 / np.sqrt(D)).then_inc(p_ready, 1)
                    act.wait_ge(pv_done, QT * (S + 1))
                    wait(act, ot_done, S)
                    act.copy(ou[:, :], o_ps[:, :]).then_inc(ou_done, 1)

            def route(f):
                for c in range(NCH):
                    act.wait_ge(rt_done, NCH * f + c + 1)
                    act.activation(sg8[:, c, :], bank[4 + c][0:NEXP, :], ACT.Sigmoid).then_inc(sig_done, 1)

            def hidden(f, i, e):
                s = FS * f + 8 * i + e
                act.wait_ge(g_ready, s + 1)
                wait(act, h_done, s - 1)
                act.activation(sg[:, e % 2, :], bank[2 * (e % 2)], ACT.Silu).then_inc(silu_done, 1)
                act.wait_ge(h_done, s + 1)
                wait(act, down_done, s - 1)
                act.copy(hh[:, e % 2, :], hf[:, e % 2, :]).then_inc(hh_done, 1)

            def experts(f):
                for e in range(8):
                    hidden(f, 0, e)
                with act.Fori(1, UNITS // 2) as i:
                    for e in range(8):
                        hidden(f, i, e)

            act.wait_ge(const_in, 64)
            act.copy(cstb[:, :, :], cst[:, 0:3, :]).then_inc(const_ready, 1)
            act.wait_ge(const_ready, 1)
            act.copy(mc[:, 0, 0, 0:1], cst[:, 0, 0:1]).then_inc(const_ready, 2)
            for l in range(2):
                x_hi(2 * l)
                qkv(l)
                attention(l)
                x_hi(2 * l + 1)
                route(l)
                experts(l)

        @block.vector
        def _(dve):
            def layernorm(p):
                def stats(c):
                    if p == 0:
                        dve.wait_ge(x_in[c], 16)
                    elif p % 2:
                        dve.wait_ge(fc_added, TT // 2 * (p // 2) + 2 * (c + 1))
                    else:
                        dve.wait_ge(added, TC * (FS * (p // 2) - NCH + c + 1))
                    for t in range(TC * c, TC * c + TC):
                        dve.bn_stats(st[:, t, :], xs[:, t, :]).then_inc(ln_stats, 1)
                    for t in range(TC * c, TC * c + TC):
                        dve.wait_ge(ln_stats, TT * p + t + 1)
                        dve.bn_aggr(mv[:, t, :], st[:, t, :]).then_inc(ln_aggr, 1)

                def lows(c):
                    for k in range(KE):
                        n = KE * (NCH * p + c) + k
                        dve.wait_ge(xth_done, n + 1)
                        dve.tensor_tensor(xt_l[:, k, CH * c:CH * c + CH], bank[n % 4],
                                          xt_h[:, k, CH * c:CH * c + CH].bitcast(F32), ALU.subtract).then_inc(xtl_done, 1)

                stats(0)
                for c in range(NCH):
                    if c + 1 < NCH:
                        stats(c + 1)
                    dve.wait_ge(ln_rstd, NCH * p + c + 1)
                    wait(dve, tr_done, KE * (NCH * p + c - 1))
                    for t in range(TC):
                        tt = TC * c + t
                        dve.tensor_scalar(xn[:, c % 2, t, :], xs[:, tt, :], mv[:, tt, 0:1], rstd[:, tt:tt + 1],
                                          ALU.subtract, ALU.mult).then_inc(xn_done, 1)
                    if c:
                        lows(c - 1)
                lows(NCH - 1)

            def split(l, c, m):
                y = split_index(l, c, m)
                a = y % 2
                dve.wait_ge(evac_done, qkv_index(l, c, m) + 1)
                wait(dve, parts_out[a], 16 * (y // 2))
                dve.tensor_copy(hml[:, a, 0, :], yb[:, a, :]).then_inc(part_step, 1)
                dve.wait_ge(part_step, 3 * y + 1)
                dve.tensor_tensor(yr[:, a, :], yb[:, a, :], hml[:, a, 0, :], ALU.subtract).then_inc(part_step, 1)
                dve.wait_ge(part_step, 3 * y + 2)
                dve.tensor_copy(hml[:, a, 1, :], yr[:, a, :]).then_inc(part_step, 1)
                dve.wait_ge(part_step, 3 * y + 3)
                dve.tensor_tensor(hml[:, a, 2, :], yr[:, a, :], hml[:, a, 1, :], ALU.subtract).then_inc(parts_done, 1)

            def qkv(l):
                for c in range(NCH):
                    for m in range(SPLIT[l]):
                        split(l, c, m)
                    if l == 0:
                        n = qkv_index(l, c, 0)
                        dve.wait_ge(vt_done, c + 1)
                        dve.tensor_copy(vp[:, TC * c:TC * c + TC, 0, 0:D],
                                        bank[4 + n % 4][:, 0:32 * TC].rearrange("p (t m) -> p t m", m=32)[:, :, D:32]).then_inc(vc_done, 1)

            def maximum(l, s, u):
                qt, half, j0, share, width, _ = SU[u]
                S = step_no(l, s)
                n = NSU * S + u
                dve.wait_ge(su_ready, n + 1)
                if qt < HALF:
                    to = mc[:, S % 2, j0:j0 + share, qt]
                else:
                    to = mab[:, S % 2, half, j0:j0 + share, qt - HALF]
                dve.tensor_reduce(to, bank[6 + n % 2][:, 0:share * width].rearrange("p (j k) -> p j k", j=share),
                                  AX.X, ALU.max).then_inc(su_used, 1)

            def maxima_parts(l, s):
                S = step_no(l, s)
                n = NSU * S + NSU - 1
                a = S % 2
                dve.wait_ge(su_used, n)
                dve.tensor_tensor(mc[:, a, :, HALF:QT], mab[:, a, 0, :, :], mab[:, a, 1, :, :], ALU.max).then_inc(mc_done, 1)
                dve.wait_ge(su_ready, n + 1)
                src = bank[6 + n % 2][0:32, 0:P]
                dve.tensor_scalar(nmx[:, a, 0, :], src, -1.0, None, ALU.mult).then_inc(nm_step, 1)
                dve.wait_ge(nm_step, 2 * S + 1)
                dve.scalar_tensor_tensor(nmr[:, a, :], src, -1.0, nmx[:, a, 0, :], ALU.mult, ALU.subtract).then_inc(su_used, 1)
                dve.wait_ge(su_used, n + 1)
                dve.tensor_copy(nmx[:, a, 1, :], nmr[:, a, :]).then_inc(nm_step, 1)
                dve.wait_ge(nm_step, 2 * S + 2)
                dve.tensor_tensor(nmx[:, a, 2, :], nmr[:, a, :], nmx[:, a, 1, :], ALU.subtract).then_inc(nm_done, 1)

            def invert(S):
                dve.wait_ge(sums_in, 16 * (S + 1))
                dve.reciprocal(sums[:, 1, :], sums[:, 0, :]).then_inc(inv_done, 1)

            def divide(l, s):
                b, g = divmod(s, G)
                dve.wait_ge(inv_in, 64 * (step_no(l, s) + 1))
                dve.tensor_tensor(ot[:, g, N * b:N * b + N], ou[:, :], inv[:, :], ALU.mult).then_inc(ot_done, 1)

            def attention(l):
                for u in range(NSU - 1):
                    maximum(l, 0, u)
                maxima_parts(l, 0)
                for s in range(STEPS):
                    if s + 1 < STEPS:
                        for u in range(NSU - 1):
                            if u == INVERT_AT and s:
                                invert(step_no(l, s - 1))
                            if u == DIVIDE_AT and s:
                                divide(l, s - 1)
                            maximum(l, s + 1, u)
                        maxima_parts(l, s + 1)
                for s in (STEPS - 2, STEPS - 1):
                    invert(step_no(l, s))
                    divide(l, s)
                for q in range(TT // 2):
                    n = TT // 2 * l + q
                    dve.wait_ge(fc_done, n + 1)
                    dve.tensor_tensor(xs[:, 2 * q:2 * q + 2, :].rearrange("p t e -> p (t e)"), bank[(6, 7, 4, 5)[q % 4]],
                                      xs[:, 2 * q:2 * q + 2, :].rearrange("p t e -> p (t e)"), ALU.add).then_inc(fc_added, 1)

            def route(f):
                def shape(ap):
                    return ap.unsqueeze(2).to_broadcast([P, TT, NEXP])

                done = [21 * 2 * f if False else f * (2 * TT + 8)]

                def link(ins):
                    done[0] += 1
                    ins.then_inc(rt_step, 1)
                    return done[0]

                for c in range(NCH):
                    dve.wait_ge(rtt_done, NCH * f + c + 1)
                    dve.tensor_copy(sc[:, TC * c:TC * c + TC, :], bank[4 + c][:, 0:TC * NEXP].rearrange("p (t e) -> p t e", e=NEXP)).then_inc(rt_used, 1)
                dve.wait_ge(rt_used, NCH * (f + 1))
                n = link(dve.tensor_tensor(sel[:, :, :], sc[:, :, :], ebb[:, :].unsqueeze(1).to_broadcast([P, TT, NEXP]), ALU.add))
                dve.wait_ge(rt_step, n)
                for t in range(TT):
                    n = link(dve.max(top[:, t, :], sel[:, t, :]))
                dve.wait_ge(rt_step, n)
                for t in range(TT):
                    n = link(dve.max_index(idx[:, t, :], top[:, t, :], sel[:, t, :]))
                dve.wait_ge(rt_step, n)
                n = link(dve.tensor_copy(idf[:, :, :], idx[:, :, 0:2]))
                dve.wait_ge(rt_step, n)
                iota_b = iota8[:, :].unsqueeze(1).to_broadcast([P, TT, NEXP])
                link(dve.tensor_tensor(eq0[:, :, :], iota_b, shape(idf[:, :, 0]), ALU.is_equal))
                n = link(dve.tensor_tensor(eq1[:, :, :], iota_b, shape(idf[:, :, 1]), ALU.is_equal))
                dve.wait_ge(rt_step, n)
                n = link(dve.tensor_tensor(eq0[:, :, :], eq0[:, :, :], eq1[:, :, :], ALU.add))
                dve.wait_ge(rt_step, n)
                n = link(dve.tensor_tensor(eq1[:, :, :], eq0[:, :, :], sc[:, :, :], ALU.mult))
                dve.wait_ge(rt_step, n)
                n = link(dve.tensor_reduce(ssum[:, 0, :], eq1[:, :, :], AX.X, ALU.add))
                dve.wait_ge(rt_step, n)
                n = link(dve.tensor_scalar(ssum[:, 1, :], ssum[:, 0, :], 1e-9, None, ALU.add))
                dve.wait_ge(rt_step, n)
                dve.reciprocal(ssum[:, 0, :], ssum[:, 1, :]).then_inc(comb_done, 1)
                dve.wait_ge(comb_done, 2 * f + 1)
                dve.tensor_tensor(comb[:, :, NEXP:UNITS], eq1[:, :, :], shape(ssum[:, 0, :]), ALU.mult).then_inc(comb_done, 1)

            def hidden(f, i, e):
                s = FS * f + 8 * i + e
                a = e % 2
                dve.wait_ge(silu_done, s + 1)
                dve.wait_ge(u_ready, s + 1)
                wait(dve, hl_done, s - 1)
                dve.tensor_tensor(hf[:, a, :], bank[2 * a + 1], sg[:, a, :], ALU.mult).then_inc(h_done, 1)
                dve.wait_ge(hh_done, s + 1)
                dve.tensor_tensor(hl[:, a, :], hf[:, a, :], hh[:, a, :].bitcast(F32), ALU.subtract).then_inc(hl_done, 1)

            def add(f, i, e):
                s = FS * f + 8 * i + e
                u, c = divmod(e, NCH)
                dve.wait_ge(down_done, s + 1)
                wait(dve, added, TC * (s - NCH + 1))
                for t in range(TC):
                    tt = TC * c + t
                    col = 2 * i + u
                    dve.scalar_tensor_tensor(xs[:, tt, :], bank[4 + 2 * (e % 2) + t // 2][:, E * (t % 2):E * (t % 2) + E],
                                             comb[:, tt, bass.ds(col, 1)], xs[:, tt, :], ALU.mult, ALU.add).then_inc(added, 1)

            def experts(f):
                for e in range(8):
                    hidden(f, 0, e)
                    if e:
                        add(f, 0, e - 1)
                with dve.Fori(1, UNITS // 2) as i:
                    for e in range(8):
                        hidden(f, i, e)
                        if e:
                            add(f, i, e - 1)
                        else:
                            add(f, i - 1, 7)
                add(f, UNITS // 2 - 1, 7)

            dve.wait_ge(const_in, 64)
            for l in range(2):
                layernorm(2 * l)
                qkv(l)
                attention(l)
                layernorm(2 * l + 1)
                route(l)
                experts(l)


def parts_of(a):
    found = []
    for _ in range(3):
        bits = a.astype(np.float32).view(np.uint32) & 0xFFFF0000
        found.append((bits >> 16).astype(np.uint16))
        a = a - bits.view(np.float32)
    return found


def shape_constants():
    p = np.arange(P)
    c = np.zeros((P, 3, P), np.float32)
    c[p, 0, p] = 1
    c[:, 1, :] = np.where(p[None, :] > p[:, None], NEG, 0)
    c[:, 2, :] = np.where(p[:, None] > p[None, :], NEG, 0)
    slope = (0.5 ** (np.arange(1, H + 1, dtype=np.float32) * 8.0 / H)).astype(np.float32)
    s = np.stack(parts_of(4 * slope) * 2)
    slopes = np.ascontiguousarray(np.broadcast_to(s[:, :, None], (ALIBI, H, N)))
    n = np.arange(N, dtype=np.float32)
    high = parts_of(np.floor(n / 8) * 8)[0]
    low = parts_of(n % 8)[0]
    one = parts_of(np.ones(N, np.float32))[0]
    krows = np.stack([high] * 3 + [low] * 3 + [one] * 3)
    iota = np.ascontiguousarray(np.broadcast_to(np.arange(NEXP, dtype=np.float32), (P, NEXP)))
    return c, slopes, krows, iota


def kernel(**inputs):
    import concourse.bacc as bacc
    from concourse.bass_utils import run_bass_kernel_spmd

    def get(name):
        return np.asarray(inputs["L0_" + name])

    w_qkv, b_qkv = get("attn_a_w_qkv"), get("attn_a_b_qkv")
    w_a = np.concatenate([w_qkv[:, E:], w_qkv[:, :P - 2 * D], w_qkv[:, :E]], 1)
    b_a = np.concatenate([b_qkv[E:], b_qkv[:P - 2 * D], b_qkv[:E]]).reshape(3, P).T

    def padded_fc(w, bias=None):
        a = np.zeros((4, 32, G, E), w.dtype)
        a[:, :D] = w.reshape(G, 4, D, E).transpose(1, 2, 0, 3)
        if bias is not None:
            a[0, D, 0] = bias
        return a.reshape(P, G, E)

    fc_a = padded_fc(get("attn_a_w_fc"), get("attn_a_b_fc"))
    fc_b = padded_fc(get("attn_b_Wo").T)
    w_b = np.concatenate([get("attn_b_Wq").T, get("attn_b_Wk").T, get("attn_b_Wv").T], 1)
    router = np.zeros((E, P), np.float32)
    router[:, :NEXP] = get("ffn_router_w").T

    def unit_weights(gate, upw, down):
        def rows(w):
            return w.T.reshape(KE, P, P).transpose(1, 0, 2).reshape(P, E)
        return np.concatenate([rows(gate), rows(upw), down.T], 1)

    sw1, sw2, sw3, w12, w3 = (get("ffn_" + n) for n in ("sw1", "sw2", "sw3", "w12", "w3"))
    units = [unit_weights(sw1[P * n:P * n + P], sw2[P * n:P * n + P], sw3[:, P * n:P * n + P]) for n in range(8)]
    units += [unit_weights(w12[n, :P], w12[n, P:], w3[n]) for n in range(NEXP)]
    consts, slopes, krows, iota = shape_constants()
    arrays = {
        "x": get("attn_a_x"), "w_a": w_a, "b_a": b_a, "fc_a": fc_a, "w_b": w_b, "fc_b": fc_b,
        "w_units": np.stack(units), "router": router, "ebias": get("ffn_expert_bias"), "iota": iota,
        "consts": consts, "slopes": slopes, "krows": krows,
    }
    nc = bacc.Bacc("TRN2", target_bir_lowering=False, num_devices=1)
    arrays = {f"{k}_dram": np.ascontiguousarray(v) for k, v in arrays.items()}
    args = [nc.dram_tensor(k, v.shape, mybir.dt.from_np(v.dtype), kind="ExternalInput").ap() for k, v in arrays.items()]
    args.append(nc.dram_tensor("out_dram", (NB, N, E), F32, kind="ExternalOutput").ap())
    program(nc, *args)
    r = run_bass_kernel_spmd(nc, [arrays], core_ids=[0])
    return r.results[0]["out_dram"]
```

```python
from contextlib import ExitStack

import numpy as np

import concourse.bass as bass
from concourse import mybir

F32 = mybir.dt.float32
F32R = mybir.dt.float32r
BF16 = mybir.dt.bfloat16
U16 = mybir.dt.uint16
U32 = mybir.dt.uint32
ACT = mybir.ActivationFunctionType
ALU = mybir.AluOpType
AX = mybir.AxisListType

NB, N, E = 2, 1024, 256
H, D = 16, 16
P = 128
T = NB * N
TT = T // P
CH = 512
NCH = T // CH
TC = CH // P
KE = E // P
G = H // 4
STEPS = NB * G
QT = N // P
HALF = QT // 2
NEXP = 8
UNITS = 16
FS = UNITS * NCH
EPS = 1e-5
NEG = -1e30
ROWS = 96
ALIBI = 6
PRODUCTS = [(0, 0), (1, 0), (2, 0), (0, 1), (1, 1), (0, 2)]
RUNS = [(0, 3), (3, 5), (5, 6)]
SBANKS = 3
KM_BANKS = (0, 1, 2)
SU_BANKS = (3, 6, 7)


def score_units():
    units = []
    for qt in range(QT):
        if qt >= HALF:
            units += [(qt, 0, j, 1, CH, False) for j in range(4)]
        width = P * (qt % HALF + 1)
        share = min(4, CH // width)
        units += [(qt, qt // HALF, j, share, width, True) for j in range(0, 4, share)]
    return units


SU = score_units()
NSU = len(SU) + 1


QUADS = [(kt, part) for kt in range(QT) for part in range(kt // HALF, 2)]
PIECES = 4 * len(QUADS)
LAST_QUAD = (QUADS.index((HALF - 1, 0)), QUADS.index((QT - 1, 1)))


def queries(q):
    kt, part = QUADS[q]
    return max(CH * part, P * kt), CH * (part + 1)


def last_quad(S, q):
    kt, part = QUADS[q]
    same = [n for n, (k, a) in enumerate(QUADS) if a == part and k % 2 == kt % 2]
    at = same.index(q)
    n = len(QUADS) * S + same[at - 1] - (len(QUADS) if at == 0 else 0)
    return n if n >= 0 else None


def units_behind_pieces(lead):
    work = np.array([queries(n // 4)[1] - queries(n // 4)[0] + P for n in range(PIECES)], float)
    at = np.append(0, np.arange(STEPS)[:, None] + np.cumsum(work)[None, :] / work.sum())
    cost = np.array([share * width + P for _, _, _, share, width, _ in SU] + [4 * CH], float)
    through = np.cumsum(cost) / cost.sum()
    behind = [[] for _ in at]
    n = 0
    for s in range(1, STEPS):
        for u, t in enumerate(s - 1 - lead + through):
            while at[n] < t - 1e-9:
                n += 1
            behind[n].append((s, u))
    return behind


UNITS_BEFORE, *UNITS_BEHIND = units_behind_pieces(0.2)
FC_BEHIND = {20 + 7 * t: t for t in range(4)}
PV_LAG = 2
PV_BEHIND = 1
INVERT_AT, DIVIDE_AT = (2, 20), (19, 33)
QKV = [[("kv", 0), ("q", 0), ("q", 1)],
       [("q", 0), ("q", 1), ("k", 0), ("k", 1), ("v", 0), ("v", 1)]]
SPLIT = [3, 4]


def qkv_index(l, c, m):
    return (l and NCH * len(QKV[0])) + len(QKV[l]) * c + m


def split_index(l, c, m):
    return (l and NCH * SPLIT[0]) + SPLIT[l] * c + m


def turns(l, s):
    return (l and len(range(s % SBANKS, STEPS, SBANKS))), s // SBANKS + 1


def wait(eng, sem, count):
    if not isinstance(count, int) or count > 0:
        eng.wait_ge(sem, count)


def split_product(pe, out, terms):
    for n, (lh, ll, rh, rl) in enumerate(terms):
        pe.matmul(out, lh, rh, start=n == 0, stop=False)
        pe.matmul(out, ll, rh, start=False, stop=False)
        last = pe.matmul(out, lh, rl, start=False, stop=n == len(terms) - 1)
    return last


def program(nc, x, w_a, b_a, fc_a, w_b, fc_b, w_units, router, ebias, iota, consts, slopes, krows, out):
    x_v = x.rearrange("b (t p) e -> p (b t) e", p=P)
    out_v = out.rearrange("b (t p) e -> p (b t) e", p=P)
    w_a_v = w_a.rearrange("(k p) m -> p k m", p=P)
    w_b_v = w_b.rearrange("(k p) m -> p k m", p=P)
    router_v = router.rearrange("(k p) m -> p k m", p=P)
    q_parts = [nc.dram_tensor(f"q_parts{l}", (NB, 3, D, H, N), BF16).ap() for l in range(2)]
    inverses = nc.dram_tensor("inverses", (2 * STEPS, 2, 4, CH), F32).ap()
    k_parts = [nc.dram_tensor(f"k_parts{l}", (NB, 3, D, (1, H)[l], N), BF16).ap() for l in range(2)]

    with ExitStack() as ctx:
        def sb(name, shape, dt):
            return ctx.enter_context(nc.sbuf_tensor(name, shape, dt))

        def sem(name):
            return ctx.enter_context(nc.semaphore(name))

        xs = sb("xs", [P, TT, E], F32)
        st = sb("st", [P, TT, 6], F32)
        mv = sb("mv", [P, TT, 2], F32)
        ve = sb("ve", [P, TT], F32)
        rstd = sb("rstd", [P, TT], F32)
        zero = sb("zero", [P, 1], F32)
        mhalf = sb("mhalf", [P, TC], F32)
        cst = sb("cst", [P, 3, P], F32)
        ident = cst[:, 0, :]
        cstb = sb("cstb", [P, 3, P], BF16)
        identb, mask_q, mask_k = cstb[:, 0, :], cstb[:, 1, :], cstb[:, 2, :]
        bias_a = sb("bias_a", [P, 3], F32)
        wraw = sb("wraw", [P, KE, 768], F32)
        wp_h, wp_l = (sb(f"wp_{n}", [P, KE, 768], F32R) for n in "hl")
        wfc = sb("wfc", [P, G, E], F32)
        rt_h, rt_l = (sb(f"rt_{n}", [P, KE, P], F32R) for n in "hl")
        vp = sb("vp", [P, TT, H, 32], F32)
        ebb = sb("ebb", [P, NEXP], F32)
        iota8 = sb("iota8", [P, NEXP], F32)
        comb = sb("comb", [P, TT, UNITS], F32)
        mc = sb("mc", [P, 2, 4, QT], F32)
        mab = sb("mab", [P, 2, 2, 4, HALF], F32)
        nmx = sb("nmx", [32, 2, 3, P], BF16)
        nmr = sb("nmr", [32, P], F32)
        xn = sb("xn", [P, 2, TC, E], F32)
        ou, inv = sb("ou", [P, N], F32), sb("inv", [P, N], F32)
        sums = sb("sums", [32, 2, 2, CH // 8], F32)

        kb = 1024
        size = [32 * kb, 32 * kb, 48 * kb]
        base = [((nc.sbuf_base + 63) // 64) * 64]
        for n in size:
            base.append(base[-1] + n)
        ctx.enter_context(nc.sbuf_tensor("arena", [P, base[-1] - nc.sbuf_base], mybir.dt.uint8))

        def region(r, plan):
            at, found = base[r], []
            for name, shape, dt in plan:
                found.append(nc.alloc_sbuf_tensor_at(name, shape, dt, offset=at))
                at += int(np.prod(shape[1:])) * (2 if dt == BF16 else 4)
            assert at <= base[r] + size[r], (name, at - base[r])
            return found

        (pt,) = region(0, [("pt", [P, 2, 4, N], F32)])
        xt_h, xt_l = region(0, [(f"xt_{n}", [P, KE, T], F32R) for n in "hl"])
        (ot,) = region(1, [("ot", [P, G, T], F32)])
        yb, yr, hml, sg8, sc, sel, eq0, eq1, top, idx, idf, ssum = region(1, [
            ("yb", [P, 2, CH], F32), ("yr", [P, 2, CH], F32), ("hml", [P, 2, 3, CH], BF16),
            ("sg8", [NEXP, NCH, CH], F32), ("sc", [P, TT, NEXP], F32), ("sel", [P, TT, NEXP], F32),
            ("eq0", [P, TT, NEXP], F32), ("eq1", [P, TT, NEXP], F32), ("top", [P, TT, 8], F32),
            ("idx", [P, TT, 8], U32), ("idf", [P, TT, 2], F32), ("ssum", [P, 2, TT], F32)])
        qs, ks = region(2, [(f"{n}s", [P, SBANKS, 4, N], BF16) for n in "qk"])
        wr, = region(2, [("wr", [P, 2, 768], F32)])
        wu_h, wu_l = (nc.alloc_sbuf_tensor_at(f"wu_{n}", [P, 2, 768], F32R, offset=base[2] + (6 + 6 * m) * kb)
                      for m, n in enumerate("hl"))
        hf, sg = (nc.alloc_sbuf_tensor_at(n, [P, 2, CH], F32, offset=base[2] + (18 + 4 * m) * kb)
                  for m, n in enumerate(("hf", "sg")))
        hh, hl = (nc.alloc_sbuf_tensor_at(n, [P, 2, CH], F32R, offset=base[2] + (26 + 4 * m) * kb)
                  for m, n in enumerate(("hh", "hl")))


        st_ps = [ctx.enter_context(nc.psum_tensor(f"st_ps{n}", [P, N], F32)) for n in range(2)]
        o_ps = ctx.enter_context(nc.psum_tensor("o_ps", [P, N], F32))
        su_ps = [ctx.enter_context(nc.psum_tensor(f"su_ps{n}", [P, CH], F32)) for n in range(2)]
        bank = [st_ps[0][:, 0:CH], st_ps[0][:, CH:N], st_ps[1][:, 0:CH], st_ps[1][:, CH:N],
                o_ps[:, 0:CH], o_ps[:, CH:N], su_ps[0][:, :], su_ps[1][:, :]]

        x_in = [sem(f"x_in{c}") for c in range(NCH)]
        const_in, wraw_in, wfc_in, unit_in = sem("const_in"), sem("wraw_in"), sem("wfc_in"), [sem("unit_in0"), sem("unit_in1")]
        const_ready, w_split, unit_split, ones_set = sem("const_ready"), sem("w_split"), sem("unit_split"), sem("ones_set")
        ln_stats, ln_aggr, ln_var, ln_rstd, xn_done = (sem(n) for n in ("ln_stats", "ln_aggr", "ln_var", "ln_rstd", "xn_done"))
        tr_done, xth_done, xtl_done = sem("tr_done"), sem("xth_done"), sem("xtl_done")
        qkv_done, evac_done, vt_done, vc_done = sem("qkv_done"), sem("evac_done"), sem("vt_done"), sem("vc_done")
        part_step, parts_done, parts_out = sem("part_step"), sem("parts_done"), [sem("parts_out0"), sem("parts_out1")]
        stk_in = [sem(f"stk_in{n}") for n in range(SBANKS)]
        max_in = [sem(f"max_in{n}") for n in range(SBANKS)]
        keys_in = [sem("keys_in0"), sem("keys_in1")]
        su_ready, su_used, mc_done, nm_step, nm_done = (sem(n) for n in ("su_ready", "su_used", "mc_done", "nm_step", "nm_done"))
        st_ready, p_ready, pv_done, ou_done, inv_done, ot_done = (
            sem(n) for n in ("st_ready", "p_ready", "pv_done", "ou_done", "inv_done", "ot_done"))
        sums_in, inv_out, inv_in = sem("sums_in"), sem("inv_out"), sem("inv_in")
        fc_done, fc_added = sem("fc_done"), sem("fc_added")
        rt_done, sig_done, rtt_done, rt_used, rt_step, comb_done = (
            sem(n) for n in ("rt_done", "sig_done", "rtt_done", "rt_used", "rt_step", "comb_done"))
        g_ready, u_ready, silu_done, h_done, hh_done, hl_done, down_done, added = (
            sem(n) for n in ("g_ready", "u_ready", "silu_done", "h_done", "hh_done", "hl_done", "down_done", "added"))
        out_sent = sem("out_sent")

        def step_no(l, s):
            return STEPS * l + s

        def stk_count(l, s):
            before, own = turns(l, s)
            return 16 * (len(RUNS) * before + (len(RUNS), 2 * len(RUNS) + 1)[l] * own)

        def max_count(l, s):
            before, own = turns(l, s)
            return 16 * 3 * (before + own)

        def batch_parts_out(l, b):
            return 16 * split_index(l, NCH // NB * (b + 1), 0) // 2

        block = ctx.enter_context(nc.Block())

        @block.sync
        def _(sp):
            for c in range(NCH):
                sp.dma_start(xs[:, TC * c:TC * c + TC, :], x_v[:, TC * c:TC * c + TC, :]).then_inc(x_in[c], 16)
                if c == 0:
                    sp.dma_start(cst[:, :, :], consts).then_inc(const_in, 16)
                    sp.dma_start(wraw[:, :, 0:3 * P], w_a_v).then_inc(wraw_in, 16)
            sp.dma_start(bias_a[:, :], b_a).then_inc(const_in, 16)
            sp.dma_start(ebb[:, :], ebias.partition_broadcast(P)).then_inc(const_in, 16)
            sp.dma_start(iota8[:, :], iota).then_inc(const_in, 16)
            sp.dma_start(wfc[:, :, :], fc_a).then_inc(wfc_in, 16)
            sp.wait_ge(w_split, 2)
            sp.dma_start(wraw[:, :, 0:P], router_v).then_inc(wraw_in, 16)
            sp.wait_ge(w_split, 4)
            sp.dma_start(wraw[:, :, :], w_b_v).then_inc(wraw_in, 16)

            def send_parts(l, c):
                for m in range(SPLIT[l]):
                    kind, mt = QKV[l][m]
                    n = split_index(l, c, m)
                    sp.wait_ge(parts_done, n + 1)
                    parts = q_parts if kind == "q" else k_parts
                    b, late = divmod(c, NCH // NB)
                    dst = parts[l][b].rearrange("t d h n -> (d h) t n")
                    rows = D if kind == "kv" else P
                    sp.dma_start(dst[rows * mt:rows * mt + rows, :, CH * late:CH * late + CH],
                                 hml[0:rows, n % 2, :, :]).then_inc(parts_out[n % 2], 16)

            def load_stack(l, s):
                b, g = divmod(s, G)
                r = s % SBANKS
                if s >= SBANKS:
                    sp.wait_ge(st_ready, PIECES * (step_no(l, s - SBANKS) + 1))
                for first, end in RUNS:
                    for stack, parts in ((qs, q_parts), (ks, k_parts))[:1 + l]:
                        if parts is q_parts:
                            src = parts[l][b, 0:end - first, :, 4 * g:4 * g + 4, :]
                        else:
                            pk = PRODUCTS[first][1]
                            src = parts[l][b, pk:pk + 1, :, 4 * g:4 * g + 4, :].to_broadcast([end - first, D, 4, N])
                        sp.dma_start(stack[D * first:D * end, r, :, :], src).then_inc(stk_in[r], 16)
                if l:
                    sp.dma_start(qs[ROWS:ROWS + ALIBI, r, :, :].bitcast(U16),
                                 slopes[:, 4 * g:4 * g + 4, :]).then_inc(stk_in[r], 16)

            def load_key_rows():
                sp.dma_start(ks[ROWS:ROWS + ALIBI + 3, :, :, :].rearrange("p r j n -> p (r j) n").bitcast(U16),
                             krows.unsqueeze(1).to_broadcast([ALIBI + 3, 4 * SBANKS, N])).then_inc(keys_in[0], 16)

            def load_keys(b):
                for first, end in RUNS:
                    pk = PRODUCTS[first][1]
                    sp.dma_start(ks[D * first:D * end, b, 0, :],
                                 k_parts[0][b, pk:pk + 1, :, 0, :].to_broadcast([end - first, D, N])).then_inc(keys_in[b], 16)
                sp.dma_start(ks[ROWS:ROWS + 3, b, 0, :].bitcast(U16), krows[ALIBI:, :]).then_inc(keys_in[b], 16)

            def send_maxima(l, s):
                r, S = s % SBANKS, step_no(l, s)
                sp.wait_ge(nm_done, S + 1)
                for part in range(3):
                    row = ROWS + l * ALIBI + part
                    sp.dma_start(qs[row:row + 1, r, :, :], nmx[:, S % 2, part, :]).then_inc(max_in[r], 16)

            def gather_sums(S, part):
                sp.wait_ge(ou_done, 2 * S + part + 1)
                sp.dma_start(sums[:, 0, part, :], ou[D:P:32, CH * part:CH * part + CH]).then_inc(sums_in, 16)

            def spread_inverses(S, part):
                sp.wait_ge(inv_done, 2 * S + part + 1)
                sp.dma_start(inverses[S, part], sums[:, 1, part, :]).then_inc(inv_out, 16)
                sp.wait_ge(inv_out, 16 * (2 * S + part + 1))
                for j in range(4):
                    sp.dma_start(inv[32 * j:32 * j + 32, CH * part:CH * part + CH],
                                 inverses[S, part, j].partition_broadcast(32)).then_inc(inv_in, 16)

            def attention(l):
                if l:
                    sp.wait_ge(added, TC * FS)
                    load_key_rows()
                for c in range(NCH - 1):
                    send_parts(l, c)
                for b in range(NB):
                    for n in range(2):
                        sp.wait_ge(parts_out[n], batch_parts_out(l, b))
                    if l == 0:
                        load_keys(b)
                    if b == 0:
                        load_stack(l, 0)
                        send_parts(l, NCH - 1)
                        for s in range(1, SBANKS):
                            load_stack(l, s)
                send_maxima(l, 0)
                for s in range(STEPS):
                    S = step_no(l, s)
                    if s:
                        spread_inverses(S - 1, 0)
                        gather_sums(S - 1, 1)
                    if s >= 1 and s + 2 < STEPS:
                        load_stack(l, s + 2)
                    if s:
                        spread_inverses(S - 1, 1)
                    gather_sums(S, 0)
                    if s + 1 < STEPS:
                        send_maxima(l, s + 1)
                S = step_no(l, STEPS - 1)
                spread_inverses(S, 0)
                gather_sums(S, 1)
                spread_inverses(S, 1)
                if l == 0:
                    sp.wait_ge(fc_done, TT // 2)
                    sp.dma_start(wfc[:, :, :], fc_b).then_inc(wfc_in, 16)

            def experts(f):
                sp.wait_ge(st_ready, PIECES * STEPS * (f + 1))
                for u in range(2):
                    sp.dma_start(wr[:, u, :], w_units[u]).then_inc(unit_in[u], 16)
                with sp.Fori(1, UNITS // 2) as i:
                    for u in range(2):
                        sp.wait_ge(unit_split, 2 * (UNITS * f) + 4 * i + 2 * u - 2)
                        sp.dma_start(wr[:, u, :], w_units[2 * i + u]).then_inc(unit_in[u], 16)

            attention(0)
            experts(0)
            attention(1)
            experts(1)
            for c in range(NCH):
                sp.wait_ge(added, TC * (2 * FS - NCH + c + 1))
                sp.dma_start(out_v[:, TC * c:TC * c + TC, :], xs[:, TC * c:TC * c + TC, :]).then_inc(out_sent, 16)
            sp.wait_ge(out_sent, 16 * NCH)

        @block.gpsimd
        def _(pool):
            pool.memset(mhalf[:, :], -0.5).then_inc(ones_set, 1)
            pool.memset(zero[:, :], 0.0).then_inc(ones_set, 1)

            def rstds(p):
                for c in range(NCH):
                    t = slice(TC * c, TC * c + TC)
                    pool.wait_ge(ln_aggr, TT * p + TC * (c + 1))
                    pool.tensor_scalar(ve[:, t], mv[:, t, 1], EPS, None, ALU.add).then_inc(ln_var, 1)
                    pool.wait_ge(ln_var, NCH * p + c + 1)
                    pool.tensor_tensor(rstd[:, t], ve[:, t], mhalf[:, :], ALU.pow).then_inc(ln_rstd, 1)

            def split_weights(n, hi, lo, m):
                pool.wait_ge(wraw_in, 16 * (n + 1))
                pool.tensor_copy(hi, wraw[:, :, 0:m]).then_inc(w_split, 1)
                pool.wait_ge(w_split, 2 * n + 1)
                pool.tensor_tensor(lo, wraw[:, :, 0:m], hi.bitcast(F32), ALU.subtract).then_inc(w_split, 1)

            def split_unit(f, u, i):
                n = UNITS * f + 2 * i + u
                pool.wait_ge(unit_in[u], 16 * (UNITS // 2 * f + i + 1))
                if not isinstance(i, int):
                    pool.wait_ge(down_done, 4 * n - 4)
                pool.tensor_tensor(wu_h[:, u, :], wr[:, u, :], zero[:, :].to_broadcast([P, 768]), ALU.subtract).then_inc(unit_split, 1)
                pool.wait_ge(unit_split, 2 * n + 1)
                pool.tensor_tensor(wu_l[:, u, :], wr[:, u, :], wu_h[:, u, :].bitcast(F32), ALU.subtract).then_inc(unit_split, 1)

            def experts(f):
                for u in range(2):
                    split_unit(f, u, 0)
                with pool.Fori(1, UNITS // 2) as i:
                    for u in range(2):
                        split_unit(f, u, i)

            pool.wait_ge(ones_set, 4)
            split_weights(0, wp_h[:, :, 0:3 * P], wp_l[:, :, 0:3 * P], 3 * P)
            rstds(0)
            split_weights(1, rt_h[:, :, :], rt_l[:, :, :], P)
            pool.wait_ge(qkv_done, NCH * len(QKV[0]))
            split_weights(2, wp_h[:, :, :], wp_l[:, :, :], 768)
            rstds(1)
            experts(0)
            rstds(2)
            rstds(3)
            experts(1)

        @block.tensor
        def _(pe):
            def transpose_chunk(p, c):
                pe.wait_ge(xn_done, TT * p + TC * (c + 1))
                for k in range(KE):
                    n = KE * (NCH * p + c) + k
                    wait(pe, xtl_done, n - 3)
                    for t in range(TC):
                        last = pe.transpose(bank[n % 4][:, P * t:P * t + P], xn[:, c % 2, t, P * k:P * k + P], ident)
                    last.then_inc(tr_done, 1)

            def qkv(l):
                pe.wait_ge(w_split, 2 + 4 * l)
                if l:
                    pe.wait_ge(added, TC * FS)
                for c in range(NCH):
                    pe.wait_ge(xtl_done, KE * (NCH * 2 * l + c + 1))
                    tok = slice(CH * c, CH * c + CH)
                    for m, (kind, mt) in enumerate(QKV[l]):
                        n = qkv_index(l, c, m)
                        out_b = bank[4 + n % 4]
                        wait(pe, evac_done, n - 3)
                        if l == 0 and (n - 4) >= 0 and (n - 4) % 3 == 0:
                            pe.wait_ge(vc_done, (n - 4) // 3 + 1)
                        if kind == "v":
                            for t in range(2):
                                tt = TC * c + 2 * mt + t
                                ts = slice(P * tt, P * tt + P)
                                last = split_product(pe, out_b[:, E * t:E * t + E], [
                                    (xt_h[:, k, ts], xt_l[:, k, ts], wp_h[:, k, 2 * E:], wp_l[:, k, 2 * E:]) for k in range(KE)])
                        else:
                            col = P * (m if l == 0 else {"q": 0, "k": 2}[kind] + mt)
                            last = split_product(pe, out_b, [
                                (wp_h[:, k, col:col + P], wp_l[:, k, col:col + P], xt_h[:, k, tok], xt_l[:, k, tok])
                                for k in range(KE)])
                        last.then_inc(qkv_done, 1)
                    if l == 0:
                        n = qkv_index(l, c, 0)
                        pe.wait_ge(evac_done, n + 1)
                        for t in range(TC):
                            last = pe.transpose(bank[4 + n % 4][:, 32 * t:32 * t + 32],
                                                yb[0:32, split_index(l, c, 0) % 2, P * t:P * t + P], ident[0:32, 0:32])
                        last.then_inc(vt_done, 1)

            def key_stack(l, s):
                return (lambda j: ks[:, s // G, 0, :]) if l == 0 else (lambda j: ks[:, s % SBANKS, j, :])

            def query_major(l, s, u):
                qt, half, j0, share, width, diagonal = SU[u]
                n = NSU * step_no(l, s) + u
                if u == 0:
                    pe.wait_ge(stk_in[s % SBANKS], stk_count(l, s))
                    if l == 0 and s == G:
                        pe.wait_ge(keys_in[1], 16 * (len(RUNS) + 1))
                out_b = bank[SU_BANKS[n % len(SU_BANKS)]]
                wait(pe, su_used, n - len(SU_BANKS) + 1)
                rows = ROWS + l * ALIBI
                for a in range(share):
                    c0 = a * width
                    last = pe.matmul(out_b[:, c0:c0 + width], qs[0:rows, s % SBANKS, j0 + a, P * qt:P * qt + P],
                                     key_stack(l, s)(j0 + a)[0:rows, CH * half:CH * half + width],
                                     start=True, stop=not diagonal)
                    if diagonal:
                        last = pe.matmul(out_b[:, c0 + width - P:c0 + width], identb, mask_q, start=False, stop=True)
                last.then_inc(su_ready, 1)

            def transpose_maxima(l, s):
                S = step_no(l, s)
                n = NSU * S + NSU - 1
                pe.wait_ge(mc_done, S + 1)
                pe.wait_ge(su_used, n - len(SU_BANKS) + 1)
                pe.transpose(bank[SU_BANKS[n % len(SU_BANKS)]][0:32, 0:P], mc[:, S % 2, :, :].rearrange("p j t -> p (j t)"), ident).then_inc(su_ready, 1)

            def key_major(l, s, q, j):
                n = PIECES * step_no(l, s) + 4 * q + j
                if q == 0 and j == 0:
                    pe.wait_ge(max_in[s % SBANKS], max_count(l, s))
                wait(pe, p_ready, n - len(KM_BANKS) + 1)
                rows = ROWS + l * ALIBI + 3
                kt, part = QUADS[q]
                lo, hi = queries(q)
                diagonal = lo == P * kt
                last = pe.matmul(bank[KM_BANKS[n % len(KM_BANKS)]][:, lo - CH * part:hi - CH * part], key_stack(l, s)(j)[0:rows, P * kt:P * kt + P],
                                 qs[0:rows, s % SBANKS, j, lo:hi], start=True, stop=not diagonal)
                if diagonal:
                    last = pe.matmul(bank[KM_BANKS[n % len(KM_BANKS)]][:, lo - CH * part:lo - CH * part + P], identb, mask_k, start=False, stop=True)
                last.then_inc(st_ready, 1)

            def values(l, s, q):
                S = step_no(l, s)
                b, g = divmod(s, G)
                kt, part = QUADS[q]
                if kt == 0:
                    wait(pe, ou_done, 2 * S - 1 + part)
                pe.wait_ge(p_ready, PIECES * S + 4 * q + 4)
                lo, hi = queries(q)
                for j in range(4):
                    last = pe.matmul(o_ps[32 * j:32 * j + 32, lo:hi], vp[:, QT * b + kt, (4 * g + j) * l, :],
                                     pt[:, kt % 2, j, lo:hi], start=kt == 0,
                                     stop=kt == (QT if part else HALF) - 1)
                last.then_inc(pv_done, 1)

            def attention(l):
                pe.wait_ge(evac_done, qkv_index(l, NCH - 1, len(QKV[l]) - 1) + 1)
                if l == 0:
                    pe.wait_ge(vc_done, NCH)
                pe.wait_ge(keys_in[0], 16 * (len(RUNS) + 1 + l))
                for u in range(NSU - 1):
                    query_major(l, 0, u)
                transpose_maxima(l, 0)
                for ahead, u in UNITS_BEFORE:
                    query_major(l, ahead, u)
                for n in range(PIECES * STEPS):
                    s, piece = divmod(n, PIECES)
                    q, j = divmod(piece, 4)
                    key_major(l, s, q, j)
                    if j == PV_BEHIND and n // 4 >= PV_LAG:
                        values(l, *divmod(n // 4 - PV_LAG, len(QUADS)))
                    for ahead, u in UNITS_BEHIND[n]:
                        if u < len(SU):
                            query_major(l, ahead, u)
                        else:
                            transpose_maxima(l, ahead)
                    if s == STEPS - 1 and piece in FC_BEHIND:
                        output_projection(l, FC_BEHIND[piece])
                for q in range(len(QUADS) - PV_LAG, len(QUADS)):
                    values(l, STEPS - 1, q)

            def output_projection(l, tt):
                n, t = divmod(TT * l + tt, 2)
                if tt == 0:
                    pe.wait_ge(wfc_in, 16 * (l + 1))
                    pe.wait_ge(su_used, NSU * STEPS * (l + 1))
                if tt in (0, QT, QT + HALF):
                    pe.wait_ge(ot_done, 2 * STEPS * l + {0: 2 * G, QT: 2 * STEPS - 1, QT + HALF: 2 * STEPS}[tt])
                if t == 0 and tt >= 4:
                    pe.wait_ge(fc_added, n - 1)
                for g in range(G):
                    last = pe.matmul(bank[6 + n % 2][:, E * t:E * t + E], ot[:, g, P * tt:P * tt + P], wfc[:, g, :],
                                     start=g == 0, stop=g == G - 1)
                if t:
                    last.then_inc(fc_done, 1)

            def route(f, c):
                if c == 0:
                    pe.wait_ge(w_split, 4)
                if c == 2:
                    pe.wait_ge(fc_added, TT // 2 * (f + 1))
                pe.wait_ge(xtl_done, KE * (NCH * (2 * f + 1) + c + 1))
                tok = slice(CH * c, CH * c + CH)
                split_product(pe, bank[4 + c], [(rt_h[:, k, :], rt_l[:, k, :], xt_h[:, k, tok], xt_l[:, k, tok])
                                                for k in range(KE)]).then_inc(rt_done, 1)

            def transpose_scores(f, c):
                pe.wait_ge(sig_done, NCH * f + c + 1)
                for t in range(TC):
                    last = pe.transpose(bank[4 + c][:, NEXP * t:NEXP * t + NEXP], sg8[:, c, P * t:P * t + P], ident[0:NEXP, 0:NEXP])
                last.then_inc(rtt_done, 1)

            def between(l):
                p = 2 * l + 1
                for tt in range(len(FC_BEHIND), QT):
                    output_projection(l, tt)
                transpose_chunk(p, 0)
                transpose_chunk(p, 1)
                for tt in range(QT, TT):
                    output_projection(l, tt)
                transpose_chunk(p, 2)
                route(l, 0)
                route(l, 1)
                transpose_chunk(p, 3)
                route(l, 2)
                route(l, 3)
                for c in range(NCH):
                    transpose_scores(l, c)

            def up(f, i, e):
                s = FS * f + 8 * i + e
                u, c = divmod(e, NCH)
                tok = slice(CH * c, CH * c + CH)
                if c == 0:
                    pe.wait_ge(unit_split, 2 * (UNITS * f + 2 * i + u + 1))
                wait(pe, h_done, s - 1)
                for a, ready in enumerate((g_ready, u_ready)):
                    split_product(pe, bank[2 * (e % 2) + a], [
                        (wu_h[:, u, E * a + P * k:E * a + P * k + P], wu_l[:, u, E * a + P * k:E * a + P * k + P],
                         xt_h[:, k, tok], xt_l[:, k, tok]) for k in range(KE)]).then_inc(ready, 1)

            def down(f, i, e):
                s = FS * f + 8 * i + e
                u, c = divmod(e, NCH)
                pe.wait_ge(hl_done, s + 1)
                wait(pe, added, TC * (s - 1))
                for t in range(TC):
                    ts = slice(P * t, P * t + P)
                    last = split_product(pe, bank[4 + 2 * (e % 2) + t // 2][:, E * (t % 2):E * (t % 2) + E], [
                        (hh[:, e % 2, ts], hl[:, e % 2, ts], wu_h[:, u, 2 * E:], wu_l[:, u, 2 * E:])])
                last.then_inc(down_done, 1)

            def experts(f):
                for e in range(8):
                    up(f, 0, e)
                    if e == 0:
                        pe.wait_ge(rt_used, NCH * (f + 1))
                    else:
                        down(f, 0, e - 1)
                with pe.Fori(1, UNITS // 2) as i:
                    for e in range(8):
                        up(f, i, e)
                        if e:
                            down(f, i, e - 1)
                        else:
                            down(f, i - 1, 7)
                down(f, UNITS // 2 - 1, 7)

            pe.wait_ge(const_ready, 3)
            pe.wait_ge(ones_set, 4)
            for l in range(2):
                for c in range(NCH):
                    transpose_chunk(2 * l, c)
                qkv(l)
                attention(l)
                between(l)
                experts(l)

        @block.scalar
        def _(act):
            def x_hi(p):
                for n in range(KE * NCH * p, KE * NCH * (p + 1)):
                    c, k = divmod(n % (KE * NCH), KE)
                    act.wait_ge(tr_done, n + 1)
                    act.copy(xt_h[:, k, CH * c:CH * c + CH], bank[n % 4]).then_inc(xth_done, 1)

            def qkv(l):
                for c in range(NCH):
                    for m, (kind, mt) in enumerate(QKV[l]):
                        n = qkv_index(l, c, m)
                        act.wait_ge(qkv_done, n + 1)
                        src = bank[4 + n % 4]
                        if kind == "v":
                            tt = TC * c + 2 * mt
                            act.copy(vp[:, tt:tt + 2, :, 0:D], src.rearrange("p (t h d) -> p t h d", t=2, d=D)).then_inc(evac_done, 1)
                            continue
                        y = split_index(l, c, m)
                        wait(act, parts_done, y - 1)
                        if l == 0 and m == 2:
                            act.wait_ge(vt_done, c + 1)
                        if l == 0:
                            act.activation(yb[:, y % 2, :], src, ACT.Identity, bias=bias_a[:, m:m + 1]).then_inc(evac_done, 1)
                        else:
                            act.copy(yb[:, y % 2, :], src).then_inc(evac_done, 1)

            def attention(l):
                def take_output(S, part):
                    act.wait_ge(pv_done, len(QUADS) * S + 1 + LAST_QUAD[part])
                    wait(act, ot_done, 2 * S + part - 1)
                    act.copy(ou[:, CH * part:CH * part + CH], o_ps[:, CH * part:CH * part + CH]).then_inc(ou_done, 1)

                for s in range(STEPS):
                    S = step_no(l, s)
                    for n in range(PIECES):
                        q, j = divmod(n, 4)
                        kt, part = QUADS[q]
                        lo, hi = queries(q)
                        i = PIECES * S + n
                        act.wait_ge(st_ready, i + 1)
                        if last_quad(S, q) is not None:
                            act.wait_ge(pv_done, last_quad(S, q) + 1)
                        act.activation(pt[:, kt % 2, j, lo:hi], bank[KM_BANKS[i % len(KM_BANKS)]][:, lo - CH * part:hi - CH * part], ACT.Exp,
                                       scale=1 / np.sqrt(D)).then_inc(p_ready, 1)
                        if s and n == 4 * PV_LAG - 1:
                            take_output(S - 1, 1)
                        if n == 4 * (LAST_QUAD[0] + PV_LAG + 1) - 1:
                            take_output(S, 0)
                take_output(step_no(l, STEPS - 1), 1)

            def route(f):
                for c in range(NCH):
                    act.wait_ge(rt_done, NCH * f + c + 1)
                    act.activation(sg8[:, c, :], bank[4 + c][0:NEXP, :], ACT.Sigmoid).then_inc(sig_done, 1)

            def hidden(f, i, e):
                s = FS * f + 8 * i + e
                act.wait_ge(g_ready, s + 1)
                wait(act, h_done, s - 1)
                act.activation(sg[:, e % 2, :], bank[2 * (e % 2)], ACT.Silu).then_inc(silu_done, 1)
                act.wait_ge(h_done, s + 1)
                wait(act, down_done, s - 1)
                act.copy(hh[:, e % 2, :], hf[:, e % 2, :]).then_inc(hh_done, 1)

            def experts(f):
                for e in range(8):
                    hidden(f, 0, e)
                with act.Fori(1, UNITS // 2) as i:
                    for e in range(8):
                        hidden(f, i, e)

            act.wait_ge(const_in, 64)
            act.copy(cstb[:, :, :], cst[:, 0:3, :]).then_inc(const_ready, 1)
            act.wait_ge(const_ready, 1)
            act.copy(mc[:, 0, 0, 0:1], cst[:, 0, 0:1]).then_inc(const_ready, 2)
            for l in range(2):
                x_hi(2 * l)
                qkv(l)
                attention(l)
                x_hi(2 * l + 1)
                route(l)
                experts(l)

        @block.vector
        def _(dve):
            def stats(p, c):
                if p == 0:
                    dve.wait_ge(x_in[c], 16)
                elif p % 2:
                    dve.wait_ge(fc_added, TT // 2 * (p // 2) + 2 * (c + 1))
                else:
                    dve.wait_ge(added, TC * (FS * (p // 2) - NCH + c + 1))
                for t in range(TC * c, TC * c + TC):
                    dve.bn_stats(st[:, t, :], xs[:, t, :]).then_inc(ln_stats, 1)
                for t in range(TC * c, TC * c + TC):
                    dve.wait_ge(ln_stats, TT * p + t + 1)
                    dve.bn_aggr(mv[:, t, :], st[:, t, :]).then_inc(ln_aggr, 1)

            def normalise(p, c):
                dve.wait_ge(ln_rstd, NCH * p + c + 1)
                wait(dve, tr_done, KE * (NCH * p + c - 1))
                for t in range(TC):
                    tt = TC * c + t
                    dve.tensor_scalar(xn[:, c % 2, t, :], xs[:, tt, :], mv[:, tt, 0:1], rstd[:, tt:tt + 1],
                                      ALU.subtract, ALU.mult).then_inc(xn_done, 1)

            def lows(p, c):
                for k in range(KE):
                    n = KE * (NCH * p + c) + k
                    dve.wait_ge(xth_done, n + 1)
                    dve.tensor_tensor(xt_l[:, k, CH * c:CH * c + CH], bank[n % 4],
                                      xt_h[:, k, CH * c:CH * c + CH].bitcast(F32), ALU.subtract).then_inc(xtl_done, 1)

            def layernorm(p):
                stats(p, 0)
                for c in range(NCH):
                    if c + 1 < NCH:
                        stats(p, c + 1)
                    normalise(p, c)
                    if c:
                        lows(p, c - 1)
                lows(p, NCH - 1)

            def split(l, c, m):
                y = split_index(l, c, m)
                a = y % 2
                dve.wait_ge(evac_done, qkv_index(l, c, m) + 1)
                wait(dve, parts_out[a], 16 * (y // 2))
                dve.tensor_copy(hml[:, a, 0, :], yb[:, a, :]).then_inc(part_step, 1)
                dve.wait_ge(part_step, 3 * y + 1)
                dve.tensor_tensor(yr[:, a, :], yb[:, a, :], hml[:, a, 0, :], ALU.subtract).then_inc(part_step, 1)
                dve.wait_ge(part_step, 3 * y + 2)
                dve.tensor_copy(hml[:, a, 1, :], yr[:, a, :]).then_inc(part_step, 1)
                dve.wait_ge(part_step, 3 * y + 3)
                dve.tensor_tensor(hml[:, a, 2, :], yr[:, a, :], hml[:, a, 1, :], ALU.subtract).then_inc(parts_done, 1)

            def qkv(l):
                for c in range(NCH):
                    for m in range(SPLIT[l]):
                        split(l, c, m)
                    if l == 0:
                        n = qkv_index(l, c, 0)
                        dve.wait_ge(vt_done, c + 1)
                        dve.tensor_copy(vp[:, TC * c:TC * c + TC, 0, 0:D],
                                        bank[4 + n % 4][:, 0:32 * TC].rearrange("p (t m) -> p t m", m=32)[:, :, D:32]).then_inc(vc_done, 1)

            def maximum(l, s, u):
                qt, half, j0, share, width, _ = SU[u]
                S = step_no(l, s)
                n = NSU * S + u
                dve.wait_ge(su_ready, n + 1)
                if qt < HALF:
                    to = mc[:, S % 2, j0:j0 + share, qt]
                else:
                    to = mab[:, S % 2, half, j0:j0 + share, qt - HALF]
                dve.tensor_reduce(to, bank[SU_BANKS[n % len(SU_BANKS)]][:, 0:share * width].rearrange("p (j k) -> p j k", j=share),
                                  AX.X, ALU.max).then_inc(su_used, 1)

            def maxima_parts(l, s):
                S = step_no(l, s)
                n = NSU * S + NSU - 1
                a = S % 2
                dve.wait_ge(su_used, n)
                dve.tensor_tensor(mc[:, a, :, HALF:QT], mab[:, a, 0, :, :], mab[:, a, 1, :, :], ALU.max).then_inc(mc_done, 1)
                dve.wait_ge(su_ready, n + 1)
                src = bank[SU_BANKS[n % len(SU_BANKS)]][0:32, 0:P]
                dve.tensor_scalar(nmx[:, a, 0, :], src, -1.0, None, ALU.mult).then_inc(nm_step, 1)
                dve.wait_ge(nm_step, 2 * S + 1)
                dve.scalar_tensor_tensor(nmr[:, :], src, -1.0, nmx[:, a, 0, :], ALU.mult, ALU.subtract).then_inc(su_used, 1)
                dve.wait_ge(su_used, n + 1)
                dve.tensor_copy(nmx[:, a, 1, :], nmr[:, :]).then_inc(nm_step, 1)
                dve.wait_ge(nm_step, 2 * S + 2)
                dve.tensor_tensor(nmx[:, a, 2, :], nmr[:, :], nmx[:, a, 1, :], ALU.subtract).then_inc(nm_done, 1)

            def invert(S, part):
                dve.wait_ge(sums_in, 16 * (2 * S + part + 1))
                dve.reciprocal(sums[:, 1, part, :], sums[:, 0, part, :]).then_inc(inv_done, 1)

            def divide(l, s, part):
                b, g = divmod(s, G)
                n0 = N * b + CH * part
                half = slice(CH * part, CH * part + CH)
                dve.wait_ge(inv_in, 64 * (2 * step_no(l, s) + part + 1))
                dve.tensor_tensor(ot[:, g, n0:n0 + CH], ou[:, half], inv[:, half], ALU.mult).then_inc(ot_done, 1)

            def attention(l):
                for u in range(NSU - 1):
                    maximum(l, 0, u)
                maxima_parts(l, 0)
                for s in range(STEPS):
                    if s + 1 < STEPS:
                        for u in range(NSU - 1):
                            for part in range(2):
                                if s and u == INVERT_AT[part]:
                                    invert(step_no(l, s - 1), part)
                                if s and u == DIVIDE_AT[part]:
                                    divide(l, s - 1, part)
                            maximum(l, s + 1, u)
                        maxima_parts(l, s + 1)
                for part in range(2):
                    invert(step_no(l, STEPS - 2), part)
                    divide(l, STEPS - 2, part)

            def add_projection(l, q):
                n = TT // 2 * l + q
                dve.wait_ge(fc_done, n + 1)
                pair = xs[:, 2 * q:2 * q + 2, :].rearrange("p t e -> p (t e)")
                dve.tensor_tensor(pair, bank[6 + n % 2], pair, ALU.add).then_inc(fc_added, 1)

            def between(l):
                p = 2 * l + 1
                add_projection(l, 0)
                invert(step_no(l, STEPS - 1), 0)
                add_projection(l, 1)
                divide(l, STEPS - 1, 0)
                stats(p, 0)
                normalise(p, 0)
                add_projection(l, 2)
                add_projection(l, 3)
                stats(p, 1)
                normalise(p, 1)
                lows(p, 0)
                lows(p, 1)
                invert(step_no(l, STEPS - 1), 1)
                add_projection(l, 4)
                add_projection(l, 5)
                divide(l, STEPS - 1, 1)
                stats(p, 2)
                normalise(p, 2)
                add_projection(l, 6)
                add_projection(l, 7)
                stats(p, 3)
                normalise(p, 3)
                lows(p, 2)
                lows(p, 3)
                for c in range(NCH):
                    dve.wait_ge(rtt_done, NCH * l + c + 1)
                    dve.tensor_copy(sc[:, TC * c:TC * c + TC, :], bank[4 + c][:, 0:TC * NEXP].rearrange("p (t e) -> p t e", e=NEXP)).then_inc(rt_used, 1)

            def route(f, stage):
                def shape(ap):
                    return ap.unsqueeze(2).to_broadcast([P, TT, NEXP])

                iota_b = iota8[:, :].unsqueeze(1).to_broadcast([P, TT, NEXP])
                done = f * (2 * TT + 8)
                if stage == 0:
                    dve.wait_ge(rt_used, NCH * (f + 1))
                    dve.tensor_tensor(sel[:, :, :], sc[:, :, :], ebb[:, :].unsqueeze(1).to_broadcast([P, TT, NEXP]), ALU.add).then_inc(rt_step, 1)
                if stage in (1, 2):
                    dve.wait_ge(rt_step, done + 1)
                    for t in range(TT // 2 * (stage - 1), TT // 2 * stage):
                        dve.max(top[:, t, :], sel[:, t, :]).then_inc(rt_step, 1)
                if stage in (3, 4):
                    dve.wait_ge(rt_step, done + 1 + TT)
                    for t in range(TT // 2 * (stage - 3), TT // 2 * (stage - 2)):
                        dve.max_index(idx[:, t, :], top[:, t, :], sel[:, t, :]).then_inc(rt_step, 1)
                if stage == 5:
                    dve.wait_ge(rt_step, done + 1 + 2 * TT)
                    dve.tensor_copy(idf[:, :, :], idx[:, :, 0:2]).then_inc(rt_step, 1)
                    dve.wait_ge(rt_step, done + 2 + 2 * TT)
                    dve.tensor_tensor(eq0[:, :, :], iota_b, shape(idf[:, :, 0]), ALU.is_equal).then_inc(rt_step, 1)
                    dve.tensor_tensor(eq1[:, :, :], iota_b, shape(idf[:, :, 1]), ALU.is_equal).then_inc(rt_step, 1)
                if stage == 6:
                    dve.wait_ge(rt_step, done + 4 + 2 * TT)
                    dve.tensor_tensor(eq0[:, :, :], eq0[:, :, :], eq1[:, :, :], ALU.add).then_inc(rt_step, 1)
                    dve.wait_ge(rt_step, done + 5 + 2 * TT)
                    dve.tensor_tensor(eq1[:, :, :], eq0[:, :, :], sc[:, :, :], ALU.mult).then_inc(rt_step, 1)
                    dve.wait_ge(rt_step, done + 6 + 2 * TT)
                    dve.tensor_reduce(ssum[:, 0, :], eq1[:, :, :], AX.X, ALU.add).then_inc(rt_step, 1)
                if stage == 7:
                    dve.wait_ge(rt_step, done + 7 + 2 * TT)
                    dve.tensor_scalar(ssum[:, 1, :], ssum[:, 0, :], 1e-9, None, ALU.add).then_inc(rt_step, 1)
                    dve.wait_ge(rt_step, done + 8 + 2 * TT)
                    dve.reciprocal(ssum[:, 0, :], ssum[:, 1, :]).then_inc(comb_done, 1)
                    dve.wait_ge(comb_done, 2 * f + 1)
                    dve.tensor_tensor(comb[:, :, NEXP:UNITS], eq1[:, :, :], shape(ssum[:, 0, :]), ALU.mult).then_inc(comb_done, 1)

            def hidden(f, i, e):
                s = FS * f + 8 * i + e
                a = e % 2
                dve.wait_ge(silu_done, s + 1)
                dve.wait_ge(u_ready, s + 1)
                wait(dve, hl_done, s - 1)
                dve.tensor_tensor(hf[:, a, :], bank[2 * a + 1], sg[:, a, :], ALU.mult).then_inc(h_done, 1)
                dve.wait_ge(hh_done, s + 1)
                dve.tensor_tensor(hl[:, a, :], hf[:, a, :], hh[:, a, :].bitcast(F32), ALU.subtract).then_inc(hl_done, 1)

            def add(f, i, e):
                s = FS * f + 8 * i + e
                u, c = divmod(e, NCH)
                dve.wait_ge(down_done, s + 1)
                wait(dve, added, TC * (s - NCH + 1))
                for t in range(TC):
                    tt = TC * c + t
                    col = 2 * i + u
                    dve.scalar_tensor_tensor(xs[:, tt, :], bank[4 + 2 * (e % 2) + t // 2][:, E * (t % 2):E * (t % 2) + E],
                                             comb[:, tt, bass.ds(col, 1)], xs[:, tt, :], ALU.mult, ALU.add).then_inc(added, 1)

            def experts(f):
                for e in range(8):
                    hidden(f, 0, e)
                    if e:
                        add(f, 0, e - 1)
                    route(f, e)
                with dve.Fori(1, UNITS // 2) as i:
                    for e in range(8):
                        hidden(f, i, e)
                        if e:
                            add(f, i, e - 1)
                        else:
                            add(f, i - 1, 7)
                add(f, UNITS // 2 - 1, 7)

            dve.memset(vp[:, :, :, :], 1.0).then_inc(ones_set, 1)
            dve.memset(comb[:, :, :], 1.0).then_inc(ones_set, 1)
            dve.wait_ge(const_in, 64)
            for l in range(2):
                layernorm(2 * l)
                qkv(l)
                attention(l)
                between(l)
                experts(l)


def parts_of(a):
    found = []
    for _ in range(3):
        bits = a.astype(np.float32).view(np.uint32) & 0xFFFF0000
        found.append((bits >> 16).astype(np.uint16))
        a = a - bits.view(np.float32)
    return found


def shape_constants():
    p = np.arange(P)
    c = np.zeros((P, 3, P), np.float32)
    c[p, 0, p] = 1
    c[:, 1, :] = np.where(p[None, :] > p[:, None], NEG, 0)
    c[:, 2, :] = np.where(p[:, None] > p[None, :], NEG, 0)
    slope = (0.5 ** (np.arange(1, H + 1, dtype=np.float32) * 8.0 / H)).astype(np.float32)
    s = np.stack(parts_of(4 * slope) * 2)
    slopes = np.ascontiguousarray(np.broadcast_to(s[:, :, None], (ALIBI, H, N)))
    n = np.arange(N, dtype=np.float32)
    high = parts_of(np.floor(n / 8) * 8)[0]
    low = parts_of(n % 8)[0]
    one = parts_of(np.ones(N, np.float32))[0]
    krows = np.stack([high] * 3 + [low] * 3 + [one] * 3)
    iota = np.ascontiguousarray(np.broadcast_to(np.arange(NEXP, dtype=np.float32), (P, NEXP)))
    return c, slopes, krows, iota


def kernel(**inputs):
    import concourse.bacc as bacc
    from concourse.bass_utils import run_bass_kernel_spmd

    def get(name):
        return np.asarray(inputs["L0_" + name])

    w_qkv, b_qkv = get("attn_a_w_qkv"), get("attn_a_b_qkv")

    def by_dim(w):
        return w.reshape(-1, H, D).transpose(0, 2, 1).reshape(w.shape)

    w_a = np.concatenate([w_qkv[:, E:], w_qkv[:, :P - 2 * D], by_dim(w_qkv[:, :E])], 1)
    b_a = np.concatenate([b_qkv[E:], b_qkv[:P - 2 * D], by_dim(b_qkv[:E])]).reshape(3, P).T

    def padded_fc(w, bias=None):
        a = np.zeros((4, 32, G, E), w.dtype)
        a[:, :D] = w.reshape(G, 4, D, E).transpose(1, 2, 0, 3)
        if bias is not None:
            a[0, D, 0] = bias
        return a.reshape(P, G, E)

    fc_a = padded_fc(get("attn_a_w_fc"), get("attn_a_b_fc"))
    fc_b = padded_fc(get("attn_b_Wo").T)
    w_b = np.concatenate([by_dim(get("attn_b_Wq").T), by_dim(get("attn_b_Wk").T), get("attn_b_Wv").T], 1)
    router = np.zeros((E, P), np.float32)
    router[:, :NEXP] = get("ffn_router_w").T

    def unit_weights(gate, upw, down):
        def rows(w):
            return w.T.reshape(KE, P, P).transpose(1, 0, 2).reshape(P, E)
        return np.concatenate([rows(gate), rows(upw), down.T], 1)

    sw1, sw2, sw3, w12, w3 = (get("ffn_" + n) for n in ("sw1", "sw2", "sw3", "w12", "w3"))
    units = [unit_weights(sw1[P * n:P * n + P], sw2[P * n:P * n + P], sw3[:, P * n:P * n + P]) for n in range(8)]
    units += [unit_weights(w12[n, :P], w12[n, P:], w3[n]) for n in range(NEXP)]
    consts, slopes, krows, iota = shape_constants()
    arrays = {
        "x": get("attn_a_x"), "w_a": w_a, "b_a": b_a, "fc_a": fc_a, "w_b": w_b, "fc_b": fc_b,
        "w_units": np.stack(units), "router": router, "ebias": get("ffn_expert_bias"), "iota": iota,
        "consts": consts, "slopes": slopes, "krows": krows,
    }
    nc = bacc.Bacc("TRN2", target_bir_lowering=False, num_devices=1)
    arrays = {f"{k}_dram": np.ascontiguousarray(v) for k, v in arrays.items()}
    args = [nc.dram_tensor(k, v.shape, mybir.dt.from_np(v.dtype), kind="ExternalInput").ap() for k, v in arrays.items()]
    args.append(nc.dram_tensor("out_dram", (NB, N, E), F32, kind="ExternalOutput").ap())
    program(nc, *args)
    r = run_bass_kernel_spmd(nc, [arrays], core_ids=[0])
    return r.results[0]["out_dram"]
```

```python
from contextlib import ExitStack

import numpy as np

import concourse.bass as bass
from concourse import mybir

F32 = mybir.dt.float32
F32R = mybir.dt.float32r
BF16 = mybir.dt.bfloat16
U16 = mybir.dt.uint16
U32 = mybir.dt.uint32
ACT = mybir.ActivationFunctionType
ALU = mybir.AluOpType
AX = mybir.AxisListType

NB, N, E = 2, 1024, 256
H, D = 16, 16
P = 128
T = NB * N
TT = T // P
CH = 512
NCH = T // CH
TC = CH // P
KE = E // P
G = H // 4
STEPS = NB * G
QT = N // P
HALF = QT // 2
NEXP = 8
UNITS = 16
FS = UNITS * NCH
EPS = 1e-5
NEG = -1e30
ROWS = 96
ALIBI = 6
PRODUCTS = [(0, 0), (1, 0), (2, 0), (0, 1), (1, 1), (0, 2)]
RUNS = [(0, 3), (3, 5), (5, 6)]
SBANKS = 3
KM_BANKS = (0, 1, 2)
SU_BANKS = (3, 6, 7)


def score_units():
    units = []
    for qt in range(QT):
        if qt >= HALF:
            units += [(qt, 0, j, 1, CH, False) for j in range(4)]
        width = P * (qt % HALF + 1)
        share = min(4, CH // width)
        units += [(qt, qt // HALF, j, share, width, True) for j in range(0, 4, share)]
    return units


SU = score_units()
NSU = len(SU) + 1


QUADS = [(kt, part) for kt in range(QT) for part in range(kt // HALF, 2)]
PIECES = 4 * len(QUADS)
LAST_QUAD = (QUADS.index((HALF - 1, 0)), QUADS.index((QT - 1, 1)))


def queries(q):
    kt, part = QUADS[q]
    return max(CH * part, P * kt), CH * (part + 1)


def last_quad(S, q):
    kt, part = QUADS[q]
    same = [n for n, (k, a) in enumerate(QUADS) if a == part and k % 2 == kt % 2]
    at = same.index(q)
    n = len(QUADS) * S + same[at - 1] - (len(QUADS) if at == 0 else 0)
    return n if n >= 0 else None


def units_behind_pieces(lead):
    work = np.array([queries(n // 4)[1] - queries(n // 4)[0] + P for n in range(PIECES)], float)
    at = np.append(0, np.arange(STEPS)[:, None] + np.cumsum(work)[None, :] / work.sum())
    cost = np.array([share * width + P for _, _, _, share, width, _ in SU] + [4 * CH], float)
    through = np.cumsum(cost) / cost.sum()
    behind = [[] for _ in at]
    n = 0
    for s in range(1, STEPS):
        for u, t in enumerate(s - 1 - lead + through):
            while at[n] < t - 1e-9:
                n += 1
            behind[n].append((s, u))
    return behind


UNITS_BEFORE, *UNITS_BEHIND = units_behind_pieces(0.2)
FC_BEHIND = {10 + 3 * t: t for t in range(QT)}
PV_LAG = 2
PV_BEHIND = 1
INVERT_AT, DIVIDE_AT = (3, 21), (14, 34)
QKV = [[("kv", 0), ("q", 0), ("q", 1)],
       [("q", 0), ("q", 1), ("k", 0), ("k", 1), ("v", 0), ("v", 1)]]
SPLIT = [3, 4]
STATS_AT = (5, 7)
PBUFS = 6


def qkv_index(l, c, m):
    return (l and NCH * len(QKV[0])) + len(QKV[l]) * c + m


def split_index(l, c, m):
    return (l and NCH * SPLIT[0]) + SPLIT[l] * c + m


def turns(l, s):
    return (l and len(range(s % SBANKS, STEPS, SBANKS))), s // SBANKS + 1


def wait(eng, sem, count):
    if not isinstance(count, int) or count > 0:
        eng.wait_ge(sem, count)


def split_product(pe, out, terms):
    for n, (lh, ll, rh, rl) in enumerate(terms):
        pe.matmul(out, lh, rh, start=n == 0, stop=False)
        pe.matmul(out, ll, rh, start=False, stop=False)
        last = pe.matmul(out, lh, rl, start=False, stop=n == len(terms) - 1)
    return last


def program(nc, x, w_a, b_a, fc_a, b_fc, w_b, fc_b, w_units, router, ebias, iota, consts, slopes, krows, out):
    x_v = x.rearrange("b (t p) e -> p (b t) e", p=P)
    out_v = out.rearrange("b (t p) e -> p (b t) e", p=P)
    w_a_v = w_a.rearrange("(k p) m -> p k m", p=P)
    w_b_v = w_b.rearrange("(k p) m -> p k m", p=P)
    router_v = router.rearrange("(k p) m -> p k m", p=P)
    q_parts = [nc.dram_tensor(f"q_parts{l}", (NB, 3, D, H, N), BF16).ap() for l in range(2)]
    inverses = nc.dram_tensor("inverses", (2 * STEPS, 2, 4, CH), F32).ap()
    k_parts = [nc.dram_tensor(f"k_parts{l}", (NB, 3, D, (1, H)[l], N), BF16).ap() for l in range(2)]

    with ExitStack() as ctx:
        def sb(name, shape, dt):
            return ctx.enter_context(nc.sbuf_tensor(name, shape, dt))

        def sem(name):
            return ctx.enter_context(nc.semaphore(name))

        xs = sb("xs", [P, TT, E], F32)
        st = sb("st", [P, TT, 6], F32)
        mv = sb("mv", [P, TT, 2], F32)
        ve = sb("ve", [P, TT], F32)
        rstd = sb("rstd", [P, TT], F32)
        zero = sb("zero", [P, 1], F32)
        mhalf = sb("mhalf", [P, TC], F32)
        cst = sb("cst", [P, 3, P], F32)
        ident = cst[:, 0, :]
        cstb = sb("cstb", [P, 3, P], BF16)
        identb, mask_q, mask_k = cstb[:, 0, :], cstb[:, 1, :], cstb[:, 2, :]
        bias_a = sb("bias_a", [P, 3], F32)
        wraw = sb("wraw", [P, KE, 768], F32)
        wp_h, wp_l = (sb(f"wp_{n}", [P, KE, 768], F32R) for n in "hl")
        wfc = sb("wfc", [P, G // 2, E], F32)
        bias_fc = sb("bias_fc", [P, E], F32)
        rt_h, rt_l = (sb(f"rt_{n}", [P, KE, P], F32R) for n in "hl")
        vp = sb("vp", [P, TT, H, 32], F32)
        ebb = sb("ebb", [P, NEXP], F32)
        iota8 = sb("iota8", [P, NEXP], F32)
        comb = sb("comb", [P, TT, UNITS], F32)
        mc = sb("mc", [P, 2, 4, QT], F32)
        mab = sb("mab", [P, 2, 2, 4, HALF], F32)
        nmx = sb("nmx", [32, 2, 3, P], BF16)
        nmr = sb("nmr", [32, P], F32)
        xn = sb("xn", [P, 2, TC, E], F32)
        ou = sb("ou", [P, N], F32)
        sums = sb("sums", [32, 2, 2, CH // 8], F32)

        kb = 1024
        size = [32 * kb, 32 * kb, 48 * kb]
        base = [((nc.sbuf_base + 63) // 64) * 64]
        for n in size:
            base.append(base[-1] + n)
        ctx.enter_context(nc.sbuf_tensor("arena", [P, base[-1] - nc.sbuf_base], mybir.dt.uint8))

        def region(r, plan):
            at, found = base[r], []
            for name, shape, dt in plan:
                found.append(nc.alloc_sbuf_tensor_at(name, shape, dt, offset=at))
                at += int(np.prod(shape[1:])) * (2 if dt == BF16 else 4)
            assert at <= base[r] + size[r], (name, at - base[r])
            return found

        (pt,) = region(0, [("pt", [P, 2, 4, N], F32)])
        xt_h, xt_l = region(0, [(f"xt_{n}", [P, KE, T], F32R) for n in "hl"])
        ot, inv = region(1, [("ot", [P, G // 2, T], F32), ("inv", [P, 2, N], F32)])
        yb, yr, hml = region(1, [("yb", [P, 2, CH], F32), ("yr", [P, 2, CH], F32), ("hml", [P, PBUFS, 3, CH], BF16)])
        sg8, sc, sel, eq0, eq1, top, idx, idf, ssum = region(1, [
            ("sg8", [NEXP, NCH, CH], F32), ("sc", [P, TT, NEXP], F32), ("sel", [P, TT, NEXP], F32),
            ("eq0", [P, TT, NEXP], F32), ("eq1", [P, TT, NEXP], F32), ("top", [P, TT, 8], F32),
            ("idx", [P, TT, 8], U32), ("idf", [P, TT, 2], F32), ("ssum", [P, 2, TT], F32)])
        qs, ks = region(2, [(f"{n}s", [P, SBANKS, 4, N], BF16) for n in "qk"])
        wr, = region(2, [("wr", [P, 2, 768], F32)])
        wu_h, wu_l = (nc.alloc_sbuf_tensor_at(f"wu_{n}", [P, 2, 768], F32R, offset=base[2] + (6 + 6 * m) * kb)
                      for m, n in enumerate("hl"))
        hf, sg = (nc.alloc_sbuf_tensor_at(n, [P, 2, CH], F32, offset=base[2] + (18 + 4 * m) * kb)
                  for m, n in enumerate(("hf", "sg")))
        hh, hl = (nc.alloc_sbuf_tensor_at(n, [P, 2, CH], F32R, offset=base[2] + (26 + 4 * m) * kb)
                  for m, n in enumerate(("hh", "hl")))


        st_ps = [ctx.enter_context(nc.psum_tensor(f"st_ps{n}", [P, N], F32)) for n in range(2)]
        o_ps = ctx.enter_context(nc.psum_tensor("o_ps", [P, N], F32))
        su_ps = [ctx.enter_context(nc.psum_tensor(f"su_ps{n}", [P, CH], F32)) for n in range(2)]
        bank = [st_ps[0][:, 0:CH], st_ps[0][:, CH:N], st_ps[1][:, 0:CH], st_ps[1][:, CH:N],
                o_ps[:, 0:CH], o_ps[:, CH:N], su_ps[0][:, :], su_ps[1][:, :]]

        x_in = [sem(f"x_in{c}") for c in range(NCH)]
        bias_in, router_in, inv_zeroed, bias_added = (sem(n) for n in ("bias_in", "router_in", "inv_zeroed", "bias_added"))
        const_in, wraw_in, wfc_in, unit_in = sem("const_in"), sem("wraw_in"), sem("wfc_in"), [sem("unit_in0"), sem("unit_in1")]
        const_ready, w_split, unit_split, ones_set = sem("const_ready"), sem("w_split"), sem("unit_split"), sem("ones_set")
        ln_stats, ln_aggr, ln_var, ln_rstd, xn_done = (sem(n) for n in ("ln_stats", "ln_aggr", "ln_var", "ln_rstd", "xn_done"))
        tr_done, xth_done, xtl_done = sem("tr_done"), sem("xth_done"), sem("xtl_done")
        qkv_done, evac_done, vt_done, vc_done = sem("qkv_done"), sem("evac_done"), sem("vt_done"), sem("vc_done")
        high_done, rest_done, mid_done, parts_done = (sem(n) for n in ("high_done", "rest_done", "mid_done", "parts_done"))
        parts_out = [sem(f"parts_out{n}") for n in range(PBUFS)]
        stk_in = [sem(f"stk_in{n}") for n in range(SBANKS)]
        max_in = [sem(f"max_in{n}") for n in range(SBANKS)]
        keys_in = [sem("keys_in0"), sem("keys_in1")]
        su_ready, su_used, mc_done, nm_step, nm_done = (sem(n) for n in ("su_ready", "su_used", "mc_done", "nm_step", "nm_done"))
        st_ready, p_ready, pv_done, ou_done, inv_done, ot_done = (
            sem(n) for n in ("st_ready", "p_ready", "pv_done", "ou_done", "inv_done", "ot_done"))
        odd_done = sem("odd_done")
        sums_in, inv_out, inv_in = sem("sums_in"), sem("inv_out"), sem("inv_in")
        fc_done, fc_added = sem("fc_done"), sem("fc_added")
        rt_done, sig_done, rtt_done, rt_used, rt_step, comb_done = (
            sem(n) for n in ("rt_done", "sig_done", "rtt_done", "rt_used", "rt_step", "comb_done"))
        g_ready, u_ready, silu_done, h_done, hh_done, hl_done, down_done, added = (
            sem(n) for n in ("g_ready", "u_ready", "silu_done", "h_done", "hh_done", "hl_done", "down_done", "added"))
        out_sent = sem("out_sent")

        def step_no(l, s):
            return STEPS * l + s

        def stk_count(l, s):
            before, own = turns(l, s)
            return 16 * (len(RUNS) * before + (len(RUNS), 2 * len(RUNS) + 1)[l] * own)

        def max_count(l, s):
            before, own = turns(l, s)
            return 16 * 3 * (before + own)

        def tr_bank(p, c, k):
            i = KE * c + k
            banks = 2 if p % 2 else 4
            return bank[4 - banks + i % banks], i - banks if i >= banks else None

        def batch_parts_out(l, b, n):
            return 16 * len(range(n, split_index(l, NCH // NB * (b + 1), 0), PBUFS))

        block = ctx.enter_context(nc.Block())

        @block.sync
        def _(sp):
            for c in range(NCH):
                sp.dma_start(xs[:, TC * c:TC * c + TC, :], x_v[:, TC * c:TC * c + TC, :]).then_inc(x_in[c], 16)
                if c == 0:
                    sp.dma_start(cst[:, :, :], consts).then_inc(const_in, 16)
                    sp.dma_start(wraw[:, :, 0:3 * P], w_a_v).then_inc(wraw_in, 16)
                    sp.dma_start(bias_a[:, :], b_a).then_inc(bias_in, 16)
            sp.dma_start(ebb[:, :], ebias.partition_broadcast(P)).then_inc(router_in, 16)
            sp.dma_start(iota8[:, :], iota).then_inc(router_in, 16)
            sp.dma_start(bias_fc[:, :], b_fc.partition_broadcast(P)).then_inc(wfc_in, 16)
            sp.dma_start(wfc[:, :, :], fc_a).then_inc(wfc_in, 16)
            sp.wait_ge(w_split, 2)
            sp.dma_start(wraw[:, :, 0:P], router_v).then_inc(wraw_in, 16)

            def send_parts(l, c):
                for m in range(SPLIT[l]):
                    kind, mt = QKV[l][m]
                    n = split_index(l, c, m)
                    sp.wait_ge(parts_done, n + 1)
                    parts = q_parts if kind == "q" else k_parts
                    b, late = divmod(c, NCH // NB)
                    dst = parts[l][b].rearrange("t d h n -> (d h) t n")
                    rows = D if kind == "kv" else P
                    sp.dma_start(dst[rows * mt:rows * mt + rows, :, CH * late:CH * late + CH],
                                 hml[0:rows, n % PBUFS, :, :]).then_inc(parts_out[n % PBUFS], 16)

            def load_stack(l, s):
                b, g = divmod(s, G)
                r = s % SBANKS
                if s >= SBANKS:
                    sp.wait_ge(st_ready, PIECES * (step_no(l, s - SBANKS) + 1))
                for first, end in RUNS:
                    for stack, parts in ((qs, q_parts), (ks, k_parts))[:1 + l]:
                        if parts is q_parts:
                            src = parts[l][b, 0:end - first, :, 4 * g:4 * g + 4, :]
                        else:
                            pk = PRODUCTS[first][1]
                            src = parts[l][b, pk:pk + 1, :, 4 * g:4 * g + 4, :].to_broadcast([end - first, D, 4, N])
                        sp.dma_start(stack[D * first:D * end, r, :, :], src).then_inc(stk_in[r], 16)
                if l:
                    sp.dma_start(qs[ROWS:ROWS + ALIBI, r, :, :].bitcast(U16),
                                 slopes[:, 4 * g:4 * g + 4, :]).then_inc(stk_in[r], 16)

            def load_key_rows():
                sp.dma_start(ks[ROWS:ROWS + ALIBI + 3, :, :, :].rearrange("p r j n -> p (r j) n").bitcast(U16),
                             krows.unsqueeze(1).to_broadcast([ALIBI + 3, 4 * SBANKS, N])).then_inc(keys_in[0], 16)

            def load_keys(b):
                for first, end in RUNS:
                    pk = PRODUCTS[first][1]
                    sp.dma_start(ks[D * first:D * end, b, 0, :],
                                 k_parts[0][b, pk:pk + 1, :, 0, :].to_broadcast([end - first, D, N])).then_inc(keys_in[b], 16)
                sp.dma_start(ks[ROWS:ROWS + 3, b, 0, :].bitcast(U16), krows[ALIBI:, :]).then_inc(keys_in[b], 16)

            def send_maxima(l, s):
                r, S = s % SBANKS, step_no(l, s)
                sp.wait_ge(nm_done, S + 1)
                for part in range(3):
                    row = ROWS + l * ALIBI + part
                    sp.dma_start(qs[row:row + 1, r, :, :], nmx[:, S % 2, part, :]).then_inc(max_in[r], 16)

            def gather_sums(S, part):
                sp.wait_ge(ou_done, 2 * S + part + 1)
                sp.dma_start(sums[:, 0, part, :], ou[D * (1 - S % 2):P:32, CH * part:CH * part + CH]).then_inc(sums_in, 16)

            def spread_inverses(S, part):
                sp.wait_ge(inv_done, 2 * S + part + 1)
                sp.dma_start(inverses[S, part], sums[:, 1, part, :]).then_inc(inv_out, 16)
                sp.wait_ge(inv_out, 16 * (2 * S + part + 1))
                if S % STEPS == 0 and part == 0:
                    sp.wait_ge(inv_zeroed, S // STEPS + 1)
                for j in range(4):
                    row = 32 * j + D * (S % 2)
                    sp.dma_start(inv[row:row + D, S % 2, CH * part:CH * part + CH],
                                 inverses[S, part, j].partition_broadcast(D)).then_inc(inv_in, 16)

            def attention(l):
                if l:
                    sp.wait_ge(added, TC * FS)
                    load_key_rows()
                for b in range(NB):
                    for c in range(NCH // NB * b, NCH // NB * (b + 1)):
                        send_parts(l, c)
                    for n in range(PBUFS):
                        sp.wait_ge(parts_out[n], batch_parts_out(l, b, n))
                    if l == 0:
                        load_keys(b)
                    if b == 0:
                        load_stack(l, 0)
                    else:
                        for s in range(1, SBANKS):
                            load_stack(l, s)
                if l == 0:
                    sp.wait_ge(w_split, 4)
                    sp.dma_start(wraw[:, :, :], w_b_v).then_inc(wraw_in, 16)
                send_maxima(l, 0)
                for s in range(STEPS):
                    S = step_no(l, s)
                    if s:
                        spread_inverses(S - 1, 0)
                        gather_sums(S - 1, 1)
                    if s >= 1 and s + 2 < STEPS:
                        load_stack(l, s + 2)
                    if s:
                        spread_inverses(S - 1, 1)
                    gather_sums(S, 0)
                    if s + 1 < STEPS:
                        send_maxima(l, s + 1)
                S = step_no(l, STEPS - 1)
                spread_inverses(S, 0)
                sp.wait_ge(st_ready, PIECES * STEPS * (l + 1))
                for u in range(2):
                    sp.dma_start(wr[:, u, :], w_units[u]).then_inc(unit_in[u], 16)
                gather_sums(S, 1)
                spread_inverses(S, 1)
                if l == 0:
                    sp.wait_ge(fc_done, TT // 2)
                    sp.dma_start(wfc[:, :, :], fc_b).then_inc(wfc_in, 16)

            def experts(f):
                with sp.Fori(1, UNITS // 2) as i:
                    for u in range(2):
                        sp.wait_ge(unit_split, 2 * (UNITS * f) + 4 * i + 2 * u - 2)
                        sp.dma_start(wr[:, u, :], w_units[2 * i + u]).then_inc(unit_in[u], 16)

            attention(0)
            experts(0)
            attention(1)
            experts(1)
            for c in range(NCH):
                sp.wait_ge(added, TC * (2 * FS - NCH + c + 1))
                sp.dma_start(out_v[:, TC * c:TC * c + TC, :], xs[:, TC * c:TC * c + TC, :]).then_inc(out_sent, 16)
            sp.wait_ge(out_sent, 16 * NCH)

        @block.gpsimd
        def _(pool):
            pool.memset(mhalf[:, :], -0.5).then_inc(ones_set, 1)
            pool.memset(zero[:, :], 0.0).then_inc(ones_set, 1)
            pool.memset(comb[:, :, :], 1.0).then_inc(ones_set, 1)

            def rstds(p, first=0, end=NCH):
                for c in range(first, end):
                    t = slice(TC * c, TC * c + TC)
                    pool.wait_ge(ln_aggr, TT * p + TC * (c + 1))
                    pool.tensor_scalar(ve[:, t], mv[:, t, 1], EPS, None, ALU.add).then_inc(ln_var, 1)
                    pool.wait_ge(ln_var, NCH * p + c + 1)
                    pool.tensor_tensor(rstd[:, t], ve[:, t], mhalf[:, :], ALU.pow).then_inc(ln_rstd, 1)

            def last_parts(l):
                for y in range(split_index(l, 0, 0), split_index(l, NCH, 0)):
                    pool.wait_ge(mid_done, y + 1)
                    pool.tensor_tensor(hml[:, y % PBUFS, 2, :], yr[:, y % 2, :], hml[:, y % PBUFS, 1, :], ALU.subtract).then_inc(parts_done, 1)

            def zero_inverses(l):
                for n in range(PBUFS):
                    pool.wait_ge(parts_out[n], batch_parts_out(l, NB - 1, n))
                pool.memset(inv[:, :, :], 0.0).then_inc(inv_zeroed, 1)

            def add_bias():
                pool.wait_ge(wfc_in, 32)
                for t in range(TT):
                    pool.wait_ge(xn_done, t + 1)
                    pool.tensor_tensor(xs[:, t, :], xs[:, t, :], bias_fc[:, :], ALU.add).then_inc(bias_added, 1)

            def split_weights(n, hi, lo, m):
                if n:
                    pool.wait_ge(wraw_in, 16 * (n + 1))
                    pool.tensor_copy(hi, wraw[:, :, 0:m]).then_inc(w_split, 1)
                pool.wait_ge(w_split, 2 * n + 1)
                pool.tensor_tensor(lo, wraw[:, :, 0:m], hi.bitcast(F32), ALU.subtract).then_inc(w_split, 1)

            def split_unit(f, u, i):
                n = UNITS * f + 2 * i + u
                pool.wait_ge(unit_in[u], 16 * (UNITS // 2 * f + i + 1))
                if not isinstance(i, int):
                    pool.wait_ge(down_done, 4 * n - 4)
                pool.tensor_tensor(wu_h[:, u, :], wr[:, u, :], zero[:, :].to_broadcast([P, 768]), ALU.subtract).then_inc(unit_split, 1)
                pool.wait_ge(unit_split, 2 * n + 1)
                pool.tensor_tensor(wu_l[:, u, :], wr[:, u, :], wu_h[:, u, :].bitcast(F32), ALU.subtract).then_inc(unit_split, 1)

            def experts(f):
                with pool.Fori(1, UNITS // 2) as i:
                    for u in range(2):
                        split_unit(f, u, i)

            pool.wait_ge(ones_set, 3)
            rstds(0, 0, 1)
            split_weights(0, wp_h[:, :, 0:3 * P], wp_l[:, :, 0:3 * P], 3 * P)
            rstds(0, 1)
            last_parts(0)
            zero_inverses(0)
            split_weights(1, rt_h[:, :, :], rt_l[:, :, :], P)
            pool.wait_ge(qkv_done, NCH * len(QKV[0]))
            split_weights(2, wp_h[:, :, :], wp_l[:, :, :], 768)
            add_bias()
            rstds(1, 0, 2)
            split_unit(0, 0, 0)
            split_unit(0, 1, 0)
            rstds(1, 2)
            experts(0)
            rstds(2)
            last_parts(1)
            zero_inverses(1)
            rstds(3, 0, 2)
            split_unit(1, 0, 0)
            split_unit(1, 1, 0)
            rstds(3, 2)
            experts(1)

        @block.tensor
        def _(pe):
            def transpose_chunk(p, c):
                pe.wait_ge(xn_done, TT * p + TC * (c + 1))
                for k in range(KE):
                    out_b, before = tr_bank(p, c, k)
                    if before is not None:
                        pe.wait_ge(xtl_done, KE * NCH * p + before + 1)
                    for t in range(TC):
                        last = pe.transpose(out_b[:, P * t:P * t + P], xn[:, c % 2, t, P * k:P * k + P], ident)
                    last.then_inc(tr_done, 1)

            def qkv(l):
                transpose_chunk(2 * l, 0)
                transpose_chunk(2 * l, 1)
                pe.wait_ge(w_split, 2 + 4 * l)
                if l:
                    pe.wait_ge(added, TC * FS)
                for c in range(NCH):
                    pe.wait_ge(xtl_done, KE * (NCH * 2 * l + c + 1))
                    tok = slice(CH * c, CH * c + CH)
                    for m, (kind, mt) in enumerate(QKV[l]):
                        n = qkv_index(l, c, m)
                        out_b = bank[4 + n % 4]
                        wait(pe, evac_done, n - 3)
                        if l == 0 and (n - 4) >= 0 and (n - 4) % 3 == 0:
                            pe.wait_ge(vc_done, (n - 4) // 3 + 1)
                        if kind == "v":
                            for t in range(2):
                                tt = TC * c + 2 * mt + t
                                ts = slice(P * tt, P * tt + P)
                                last = split_product(pe, out_b[:, E * t:E * t + E], [
                                    (xt_h[:, k, ts], xt_l[:, k, ts], wp_h[:, k, 2 * E:], wp_l[:, k, 2 * E:]) for k in range(KE)])
                        else:
                            col = P * (m if l == 0 else {"q": 0, "k": 2}[kind] + mt)
                            last = split_product(pe, out_b, [
                                (wp_h[:, k, col:col + P], wp_l[:, k, col:col + P], xt_h[:, k, tok], xt_l[:, k, tok])
                                for k in range(KE)])
                        last.then_inc(qkv_done, 1)
                    if l == 0:
                        n = qkv_index(l, c, 0)
                        pe.wait_ge(evac_done, n + 1)
                        for t in range(TC):
                            last = pe.transpose(bank[4 + n % 4][:, 32 * t:32 * t + 32],
                                                yb[0:32, split_index(l, c, 0) % 2, P * t:P * t + P], ident[0:32, 0:32])
                        last.then_inc(vt_done, 1)
                    if c + 2 < NCH:
                        transpose_chunk(2 * l, c + 2)

            def key_stack(l, s):
                return (lambda j: ks[:, s // G, 0, :]) if l == 0 else (lambda j: ks[:, s % SBANKS, j, :])

            def query_major(l, s, u):
                qt, half, j0, share, width, diagonal = SU[u]
                n = NSU * step_no(l, s) + u
                if u == 0:
                    pe.wait_ge(stk_in[s % SBANKS], stk_count(l, s))
                    if l == 0 and s == G:
                        pe.wait_ge(keys_in[1], 16 * (len(RUNS) + 1))
                out_b = bank[SU_BANKS[n % len(SU_BANKS)]]
                wait(pe, su_used, n - len(SU_BANKS) + 1)
                rows = ROWS + l * ALIBI
                for a in range(share):
                    c0 = a * width
                    last = pe.matmul(out_b[:, c0:c0 + width], qs[0:rows, s % SBANKS, j0 + a, P * qt:P * qt + P],
                                     key_stack(l, s)(j0 + a)[0:rows, CH * half:CH * half + width],
                                     start=True, stop=not diagonal)
                    if diagonal:
                        last = pe.matmul(out_b[:, c0 + width - P:c0 + width], identb, mask_q, start=False, stop=True)
                last.then_inc(su_ready, 1)

            def transpose_maxima(l, s):
                S = step_no(l, s)
                n = NSU * S + NSU - 1
                pe.wait_ge(mc_done, S + 1)
                pe.wait_ge(su_used, n - len(SU_BANKS) + 1)
                pe.transpose(bank[SU_BANKS[n % len(SU_BANKS)]][0:32, 0:P], mc[:, S % 2, :, :].rearrange("p j t -> p (j t)"), ident).then_inc(su_ready, 1)

            def key_major(l, s, q, j):
                n = PIECES * step_no(l, s) + 4 * q + j
                if q == 0 and j == 0:
                    pe.wait_ge(max_in[s % SBANKS], max_count(l, s))
                wait(pe, p_ready, n - len(KM_BANKS) + 1)
                rows = ROWS + l * ALIBI + 3
                kt, part = QUADS[q]
                lo, hi = queries(q)
                diagonal = lo == P * kt
                last = pe.matmul(bank[KM_BANKS[n % len(KM_BANKS)]][:, lo - CH * part:hi - CH * part], key_stack(l, s)(j)[0:rows, P * kt:P * kt + P],
                                 qs[0:rows, s % SBANKS, j, lo:hi], start=True, stop=not diagonal)
                if diagonal:
                    last = pe.matmul(bank[KM_BANKS[n % len(KM_BANKS)]][:, lo - CH * part:lo - CH * part + P], identb, mask_k, start=False, stop=True)
                last.then_inc(st_ready, 1)

            def values(l, s, q):
                S = step_no(l, s)
                b, g = divmod(s, G)
                kt, part = QUADS[q]
                if kt == 0:
                    wait(pe, ou_done, 2 * S - 1 + part)
                pe.wait_ge(p_ready, PIECES * S + 4 * q + 4)
                lo, hi = queries(q)
                for j in range(4):
                    last = pe.matmul(o_ps[32 * j:32 * j + 32, lo:hi], vp[:, QT * b + kt, 4 * g + j if l else 4 * (g % 2), :],
                                     pt[:, kt % 2, j, lo:hi], start=kt == 0,
                                     stop=kt == (QT if part else HALF) - 1)
                last.then_inc(pv_done, 1)

            def attention(l):
                pe.wait_ge(evac_done, qkv_index(l, NCH - 1, len(QKV[l]) - 1) + 1)
                if l == 0:
                    pe.wait_ge(vc_done, NCH)
                pe.wait_ge(keys_in[0], 16 * (len(RUNS) + 1 + l))
                for u in range(NSU - 1):
                    query_major(l, 0, u)
                transpose_maxima(l, 0)
                for ahead, u in UNITS_BEFORE:
                    query_major(l, ahead, u)
                for n in range(PIECES * STEPS):
                    s, piece = divmod(n, PIECES)
                    q, j = divmod(piece, 4)
                    key_major(l, s, q, j)
                    if j == PV_BEHIND and n // 4 >= PV_LAG:
                        values(l, *divmod(n // 4 - PV_LAG, len(QUADS)))
                    for ahead, u in UNITS_BEHIND[n]:
                        if u < len(SU):
                            query_major(l, ahead, u)
                        else:
                            transpose_maxima(l, ahead)
                    if s == STEPS - 1 and piece in FC_BEHIND:
                        output_projection(l, FC_BEHIND[piece])
                for q in range(len(QUADS) - PV_LAG, len(QUADS)):
                    values(l, STEPS - 1, q)

            def output_projection(l, tt):
                n, t = divmod(TT * l + tt, 2)
                if tt == 0:
                    pe.wait_ge(wfc_in, 16 * (l + 2))
                    pe.wait_ge(su_used, NSU * STEPS * (l + 1))
                if tt in (0, QT, QT + HALF):
                    pe.wait_ge(ot_done, 2 * STEPS * l + {0: 2 * G, QT: 2 * STEPS - 1, QT + HALF: 2 * STEPS}[tt])
                if t == 0 and tt >= 4:
                    pe.wait_ge(fc_added, n - 1)
                for i in range(G // 2):
                    last = pe.matmul(bank[6 + n % 2][:, E * t:E * t + E], ot[:, i, P * tt:P * tt + P], wfc[:, i, :],
                                     start=i == 0, stop=i == G // 2 - 1)
                if t:
                    last.then_inc(fc_done, 1)

            def route(f, c):
                if c == 0:
                    pe.wait_ge(w_split, 4)
                    pe.wait_ge(ou_done, 2 * STEPS * (f + 1))
                if c == 2:
                    pe.wait_ge(fc_added, TT // 2 * (f + 1))
                pe.wait_ge(xtl_done, KE * (NCH * (2 * f + 1) + c + 1))
                tok = slice(CH * c, CH * c + CH)
                split_product(pe, bank[4 + c], [(rt_h[:, k, :], rt_l[:, k, :], xt_h[:, k, tok], xt_l[:, k, tok])
                                                for k in range(KE)]).then_inc(rt_done, 1)

            def transpose_scores(f, c):
                pe.wait_ge(sig_done, NCH * f + c + 1)
                for t in range(TC):
                    last = pe.transpose(bank[4 + c][:, NEXP * t:NEXP * t + NEXP], sg8[:, c, P * t:P * t + P], ident[0:NEXP, 0:NEXP])
                last.then_inc(rtt_done, 1)

            def between(l):
                p = 2 * l + 1
                for c in range(2):
                    transpose_chunk(p, c)
                    output_projection(l, QT + 2 * c)
                    output_projection(l, QT + 2 * c + 1)
                up(l, 0, 0)
                route(l, 0)
                route(l, 1)
                transpose_chunk(p, 2)
                for tt in range(QT + HALF, TT):
                    output_projection(l, tt)
                route(l, 2)
                transpose_chunk(p, 3)
                route(l, 3)
                up(l, 0, 1)
                for c in range(NCH):
                    transpose_scores(l, c)

            def up(f, i, e):
                s = FS * f + 8 * i + e
                u, c = divmod(e, NCH)
                tok = slice(CH * c, CH * c + CH)
                if c == 0:
                    pe.wait_ge(unit_split, 2 * (UNITS * f + 2 * i + u + 1))
                wait(pe, h_done, s - 1)
                for a, ready in enumerate((g_ready, u_ready)):
                    split_product(pe, bank[2 * (e % 2) + a], [
                        (wu_h[:, u, E * a + P * k:E * a + P * k + P], wu_l[:, u, E * a + P * k:E * a + P * k + P],
                         xt_h[:, k, tok], xt_l[:, k, tok]) for k in range(KE)]).then_inc(ready, 1)

            def down(f, i, e):
                s = FS * f + 8 * i + e
                u, c = divmod(e, NCH)
                pe.wait_ge(hl_done, s + 1)
                wait(pe, added, TC * (s - 1))
                for t in range(TC):
                    ts = slice(P * t, P * t + P)
                    last = split_product(pe, bank[4 + 2 * (e % 2) + t // 2][:, E * (t % 2):E * (t % 2) + E], [
                        (hh[:, e % 2, ts], hl[:, e % 2, ts], wu_h[:, u, 2 * E:], wu_l[:, u, 2 * E:])])
                last.then_inc(down_done, 1)

            def experts(f):
                for e in range(8):
                    if e > 1:
                        up(f, 0, e)
                    if e == 0:
                        pe.wait_ge(rt_used, NCH * (f + 1))
                    else:
                        down(f, 0, e - 1)
                with pe.Fori(1, UNITS // 2) as i:
                    for e in range(8):
                        up(f, i, e)
                        if e:
                            down(f, i, e - 1)
                        else:
                            down(f, i - 1, 7)
                down(f, UNITS // 2 - 1, 7)

            pe.wait_ge(const_ready, 3)
            pe.wait_ge(ones_set, 4)
            for l in range(2):
                qkv(l)
                attention(l)
                between(l)
                experts(l)

        @block.scalar
        def _(act):
            def x_hi(p, c):
                for k in range(KE):
                    n = KE * (NCH * p + c) + k
                    act.wait_ge(tr_done, n + 1)
                    act.copy(xt_h[:, k, CH * c:CH * c + CH], tr_bank(p, c, k)[0]).then_inc(xth_done, 1)

            def qkv(l):
                x_hi(2 * l, 0)
                x_hi(2 * l, 1)
                for c in range(NCH):
                    for m, (kind, mt) in enumerate(QKV[l]):
                        n = qkv_index(l, c, m)
                        act.wait_ge(qkv_done, n + 1)
                        src = bank[4 + n % 4]
                        if kind == "v":
                            tt = TC * c + 2 * mt
                            values = src.rearrange("p (t g o m) -> p t g o m", t=2, o=2, m=4 * D)
                            for t in range(2):
                                for odd in range(2):
                                    dst = vp[:, tt + t, :, D * odd:D * odd + D].rearrange("p (g o j) d -> p g o j d", o=2, j=4)
                                    last = act.copy(dst[:, :, odd, :, :],
                                                    values[:, t, :, odd, :].rearrange("p g (j d) -> p g j d", d=D))
                            last.then_inc(evac_done, 1)
                            continue
                        y = split_index(l, c, m)
                        bias = {"bias": bias_a[:, m:m + 1]} if l == 0 else {}
                        wait(act, parts_out[y % PBUFS], 16 * (y // PBUFS))
                        act.activation(hml[:, y % PBUFS, 0, :], src, ACT.Identity, **bias).then_inc(high_done, 1)
                        wait(act, rest_done, y - 1)
                        if l == 0 and m == 2:
                            act.wait_ge(vt_done, c + 1)
                        act.activation(yb[:, y % 2, :], src, ACT.Identity, **bias).then_inc(evac_done, 1)
                    if c + 2 < NCH:
                        x_hi(2 * l, c + 2)

            def attention(l):
                def take_output(S, part):
                    act.wait_ge(pv_done, len(QUADS) * S + 1 + LAST_QUAD[part])
                    wait(act, ot_done, 2 * S + part - 1)
                    act.copy(ou[:, CH * part:CH * part + CH], o_ps[:, CH * part:CH * part + CH]).then_inc(ou_done, 1)

                for s in range(STEPS):
                    S = step_no(l, s)
                    for n in range(PIECES):
                        q, j = divmod(n, 4)
                        kt, part = QUADS[q]
                        lo, hi = queries(q)
                        i = PIECES * S + n
                        act.wait_ge(st_ready, i + 1)
                        if last_quad(S, q) is not None:
                            act.wait_ge(pv_done, last_quad(S, q) + 1)
                        act.activation(pt[:, kt % 2, j, lo:hi], bank[KM_BANKS[i % len(KM_BANKS)]][:, lo - CH * part:hi - CH * part], ACT.Exp,
                                       scale=1 / np.sqrt(D)).then_inc(p_ready, 1)
                        if s and n == 4 * PV_LAG - 1:
                            take_output(S - 1, 1)
                        if n == 4 * (LAST_QUAD[0] + PV_LAG + 1) - 1:
                            take_output(S, 0)
                take_output(step_no(l, STEPS - 1), 1)

            def route(f, first, end):
                for c in range(first, end):
                    act.wait_ge(rt_done, NCH * f + c + 1)
                    act.activation(sg8[:, c, :], bank[4 + c][0:NEXP, :], ACT.Sigmoid).then_inc(sig_done, 1)

            def hidden(f, i, e):
                s = FS * f + 8 * i + e
                act.wait_ge(g_ready, s + 1)
                wait(act, h_done, s - 1)
                act.activation(sg[:, e % 2, :], bank[2 * (e % 2)], ACT.Silu).then_inc(silu_done, 1)
                act.wait_ge(h_done, s + 1)
                wait(act, down_done, s - 1)
                act.copy(hh[:, e % 2, :], hf[:, e % 2, :]).then_inc(hh_done, 1)

            def experts(f):
                for e in range(8):
                    hidden(f, 0, e)
                with act.Fori(1, UNITS // 2) as i:
                    for e in range(8):
                        hidden(f, i, e)

            act.wait_ge(ones_set, 3)
            act.activation(vp[:, :, :, :].rearrange("p t h d -> p (t h d)"), mhalf[:, 0:1].to_broadcast([P, TT * H * 32]),
                           ACT.Identity, scale=-2.0).then_inc(ones_set, 1)
            act.wait_ge(const_in, 16)
            act.copy(cstb[:, :, :], cst[:, 0:3, :]).then_inc(const_ready, 1)
            act.wait_ge(const_ready, 1)
            act.copy(mc[:, 0, 0, 0:1], cst[:, 0, 0:1]).then_inc(const_ready, 2)
            act.wait_ge(wraw_in, 16)
            act.copy(wp_h[:, :, 0:3 * P], wraw[:, :, 0:3 * P]).then_inc(w_split, 1)
            act.wait_ge(bias_in, 16)
            for l in range(2):
                qkv(l)
                attention(l)
                for c in range(3):
                    x_hi(2 * l + 1, c)
                route(l, 0, 2)
                x_hi(2 * l + 1, 3)
                route(l, 2, NCH)
                experts(l)

        @block.vector
        def _(dve):
            def stats(p, c):
                if p == 0:
                    dve.wait_ge(x_in[c], 16)
                elif p % 2:
                    dve.wait_ge(fc_added, TT // 2 * (p // 2) + 2 * (c + 1))
                else:
                    dve.wait_ge(added, TC * (FS * (p // 2) - NCH + c + 1))
                for t in range(TC * c, TC * c + TC):
                    dve.bn_stats(st[:, t, :], xs[:, t, :]).then_inc(ln_stats, 1)
                for t in range(TC * c, TC * c + TC):
                    dve.wait_ge(ln_stats, TT * p + t + 1)
                    dve.bn_aggr(mv[:, t, :], st[:, t, :]).then_inc(ln_aggr, 1)

            def normalise(p, c):
                dve.wait_ge(ln_rstd, NCH * p + c + 1)
                wait(dve, tr_done, KE * (NCH * p + c - 1))
                for t in range(TC):
                    tt = TC * c + t
                    dve.tensor_scalar(xn[:, c % 2, t, :], xs[:, tt, :], mv[:, tt, 0:1], rstd[:, tt:tt + 1],
                                      ALU.subtract, ALU.mult).then_inc(xn_done, 1)

            def lows(p, c):
                for k in range(KE):
                    n = KE * (NCH * p + c) + k
                    dve.wait_ge(xth_done, n + 1)
                    dve.tensor_tensor(xt_l[:, k, CH * c:CH * c + CH], tr_bank(p, c, k)[0],
                                      xt_h[:, k, CH * c:CH * c + CH].bitcast(F32), ALU.subtract).then_inc(xtl_done, 1)

            def split(l, c, m):
                y = split_index(l, c, m)
                dve.wait_ge(evac_done, qkv_index(l, c, m) + 1)
                dve.wait_ge(high_done, y + 1)
                wait(dve, parts_done, y - 1)
                dve.tensor_tensor(yr[:, y % 2, :], yb[:, y % 2, :], hml[:, y % PBUFS, 0, :], ALU.subtract).then_inc(rest_done, 1)
                dve.wait_ge(rest_done, y + 1)
                dve.tensor_copy(hml[:, y % PBUFS, 1, :], yr[:, y % 2, :]).then_inc(mid_done, 1)

            def split_chunk(l, c):
                for m in range(SPLIT[l]):
                    split(l, c, m)
                if l == 0:
                    n = qkv_index(l, c, 0)
                    dve.wait_ge(vt_done, c + 1)
                    src = bank[4 + n % 4][:, 0:32 * TC].rearrange("p (t m) -> p t m", m=32)[:, :, D:32]
                    dve.tensor_copy(vp[:, TC * c:TC * c + TC, 0, 0:D], src)
                    dve.tensor_copy(vp[:, TC * c:TC * c + TC, 4, D:32], src).then_inc(vc_done, 1)

            def qkv(l):
                p = 2 * l
                if l == 0:
                    stats(p, 0)
                    stats(p, 1)
                    normalise(p, 0)
                stats(p, 2)
                normalise(p, 1)
                lows(p, 0)
                stats(p, 3)
                lows(p, 1)
                normalise(p, 2)
                split_chunk(l, 0)
                lows(p, 2)
                normalise(p, 3)
                split_chunk(l, 1)
                lows(p, 3)
                split_chunk(l, 2)
                split_chunk(l, 3)

            def maximum(l, s, u):
                qt, half, j0, share, width, _ = SU[u]
                S = step_no(l, s)
                n = NSU * S + u
                dve.wait_ge(su_ready, n + 1)
                if qt < HALF:
                    to = mc[:, S % 2, j0:j0 + share, qt]
                else:
                    to = mab[:, S % 2, half, j0:j0 + share, qt - HALF]
                dve.tensor_reduce(to, bank[SU_BANKS[n % len(SU_BANKS)]][:, 0:share * width].rearrange("p (j k) -> p j k", j=share),
                                  AX.X, ALU.max).then_inc(su_used, 1)

            def maxima_parts(l, s):
                S = step_no(l, s)
                n = NSU * S + NSU - 1
                a = S % 2
                dve.wait_ge(su_used, n)
                dve.tensor_tensor(mc[:, a, :, HALF:QT], mab[:, a, 0, :, :], mab[:, a, 1, :, :], ALU.max).then_inc(mc_done, 1)
                dve.wait_ge(su_ready, n + 1)
                src = bank[SU_BANKS[n % len(SU_BANKS)]][0:32, 0:P]
                dve.tensor_scalar(nmx[:, a, 0, :], src, -1.0, None, ALU.mult).then_inc(nm_step, 1)
                dve.wait_ge(nm_step, 2 * S + 1)
                dve.scalar_tensor_tensor(nmr[:, :], src, -1.0, nmx[:, a, 0, :], ALU.mult, ALU.subtract).then_inc(su_used, 1)
                dve.wait_ge(su_used, n + 1)
                dve.tensor_copy(nmx[:, a, 1, :], nmr[:, :]).then_inc(nm_step, 1)
                dve.wait_ge(nm_step, 2 * S + 2)
                dve.tensor_tensor(nmx[:, a, 2, :], nmr[:, :], nmx[:, a, 1, :], ALU.subtract).then_inc(nm_done, 1)

            def invert(S, part):
                dve.wait_ge(sums_in, 16 * (2 * S + part + 1))
                dve.reciprocal(sums[:, 1, part, :], sums[:, 0, part, :]).then_inc(inv_done, 1)

            def divide(l, s, part):
                b, g = divmod(s, G)
                n0 = N * b + CH * part
                half = slice(CH * part, CH * part + CH)
                dve.wait_ge(inv_in, 64 * (2 * step_no(l, s) + part + 1))
                own = ot[:, g // 2, n0:n0 + CH]
                if g % 2 == 0:
                    dve.tensor_tensor(own, ou[:, half], inv[:, 0, half], ALU.mult).then_inc(ot_done, 1)
                else:
                    n = 2 * (STEPS // 2 * l + s // 2) + part
                    dve.tensor_tensor(ou[:, half], ou[:, half], inv[:, 1, half], ALU.mult).then_inc(odd_done, 1)
                    dve.wait_ge(odd_done, n + 1)
                    dve.tensor_tensor(own, own, ou[:, half], ALU.add).then_inc(ot_done, 1)

            def attention(l):
                for u in range(NSU - 1):
                    maximum(l, 0, u)
                maxima_parts(l, 0)
                for s in range(STEPS):
                    if s + 1 < STEPS:
                        for u in range(NSU - 1):
                            for part in range(2):
                                if s and u == INVERT_AT[part]:
                                    invert(step_no(l, s - 1), part)
                                if s and u == DIVIDE_AT[part]:
                                    divide(l, s - 1, part)
                            maximum(l, s + 1, u)
                        maxima_parts(l, s + 1)
                invert(step_no(l, STEPS - 2), 0)
                divide(l, STEPS - 2, 0)
                invert(step_no(l, STEPS - 2), 1)

            def add_projection(l, q):
                n = TT // 2 * l + q
                dve.wait_ge(fc_done, n + 1)
                if l == 0 and q == 0:
                    dve.wait_ge(bias_added, TT)
                pair = xs[:, 2 * q:2 * q + 2, :].rearrange("p t e -> p (t e)")
                dve.tensor_tensor(pair, bank[6 + n % 2], pair, ALU.add).then_inc(fc_added, 1)

            def between(l):
                p = 2 * l + 1
                add_projection(l, 0)
                add_projection(l, 1)
                stats(p, 0)
                divide(l, STEPS - 2, 1)
                normalise(p, 0)
                add_projection(l, 2)
                add_projection(l, 3)
                stats(p, 1)
                normalise(p, 1)
                invert(step_no(l, STEPS - 1), 0)
                divide(l, STEPS - 1, 0)
                lows(p, 0)
                add_projection(l, 4)
                invert(step_no(l, STEPS - 1), 1)
                lows(p, 1)
                add_projection(l, 5)
                stats(p, 2)
                normalise(p, 2)
                divide(l, STEPS - 1, 1)
                add_projection(l, 6)
                add_projection(l, 7)
                stats(p, 3)
                lows(p, 2)
                normalise(p, 3)
                lows(p, 3)
                for c in range(NCH):
                    dve.wait_ge(rtt_done, NCH * l + c + 1)
                    dve.tensor_copy(sc[:, TC * c:TC * c + TC, :], bank[4 + c][:, 0:TC * NEXP].rearrange("p (t e) -> p t e", e=NEXP)).then_inc(rt_used, 1)

            def route(f, stage):
                def shape(ap):
                    return ap.unsqueeze(2).to_broadcast([P, TT, NEXP])

                iota_b = iota8[:, :].unsqueeze(1).to_broadcast([P, TT, NEXP])
                done = f * (2 * TT + 8)
                if stage == 0:
                    dve.wait_ge(router_in, 32)
                    dve.wait_ge(rt_used, NCH * (f + 1))
                    dve.tensor_tensor(sel[:, :, :], sc[:, :, :], ebb[:, :].unsqueeze(1).to_broadcast([P, TT, NEXP]), ALU.add).then_inc(rt_step, 1)
                if stage in (1, 2):
                    dve.wait_ge(rt_step, done + 1)
                    for t in range(TT // 2 * (stage - 1), TT // 2 * stage):
                        dve.max(top[:, t, :], sel[:, t, :]).then_inc(rt_step, 1)
                if stage in (3, 4):
                    dve.wait_ge(rt_step, done + 1 + TT)
                    for t in range(TT // 2 * (stage - 3), TT // 2 * (stage - 2)):
                        dve.max_index(idx[:, t, :], top[:, t, :], sel[:, t, :]).then_inc(rt_step, 1)
                if stage == 5:
                    dve.wait_ge(rt_step, done + 1 + 2 * TT)
                    dve.tensor_copy(idf[:, :, :], idx[:, :, 0:2]).then_inc(rt_step, 1)
                    dve.wait_ge(rt_step, done + 2 + 2 * TT)
                    dve.tensor_tensor(eq0[:, :, :], iota_b, shape(idf[:, :, 0]), ALU.is_equal).then_inc(rt_step, 1)
                    dve.tensor_tensor(eq1[:, :, :], iota_b, shape(idf[:, :, 1]), ALU.is_equal).then_inc(rt_step, 1)
                if stage == 6:
                    dve.wait_ge(rt_step, done + 4 + 2 * TT)
                    dve.tensor_tensor(eq0[:, :, :], eq0[:, :, :], eq1[:, :, :], ALU.add).then_inc(rt_step, 1)
                    dve.wait_ge(rt_step, done + 5 + 2 * TT)
                    dve.tensor_tensor(eq1[:, :, :], eq0[:, :, :], sc[:, :, :], ALU.mult).then_inc(rt_step, 1)
                    dve.wait_ge(rt_step, done + 6 + 2 * TT)
                    dve.tensor_reduce(ssum[:, 0, :], eq1[:, :, :], AX.X, ALU.add).then_inc(rt_step, 1)
                if stage == 7:
                    dve.wait_ge(rt_step, done + 7 + 2 * TT)
                    dve.tensor_scalar(ssum[:, 1, :], ssum[:, 0, :], 1e-9, None, ALU.add).then_inc(rt_step, 1)
                    dve.wait_ge(rt_step, done + 8 + 2 * TT)
                    dve.reciprocal(ssum[:, 0, :], ssum[:, 1, :]).then_inc(comb_done, 1)
                    dve.wait_ge(comb_done, 2 * f + 1)
                    dve.tensor_tensor(comb[:, :, NEXP:UNITS], eq1[:, :, :], shape(ssum[:, 0, :]), ALU.mult).then_inc(comb_done, 1)

            def hidden(f, i, e):
                s = FS * f + 8 * i + e
                a = e % 2
                dve.wait_ge(silu_done, s + 1)
                dve.wait_ge(u_ready, s + 1)
                wait(dve, hl_done, s - 1)
                dve.tensor_tensor(hf[:, a, :], bank[2 * a + 1], sg[:, a, :], ALU.mult).then_inc(h_done, 1)
                dve.wait_ge(hh_done, s + 1)
                dve.tensor_tensor(hl[:, a, :], hf[:, a, :], hh[:, a, :].bitcast(F32), ALU.subtract).then_inc(hl_done, 1)

            def add(f, i, e):
                s = FS * f + 8 * i + e
                u, c = divmod(e, NCH)
                dve.wait_ge(down_done, s + 1)
                wait(dve, added, TC * (s - NCH + 1))
                for t in range(TC):
                    tt = TC * c + t
                    col = 2 * i + u
                    dve.scalar_tensor_tensor(xs[:, tt, :], bank[4 + 2 * (e % 2) + t // 2][:, E * (t % 2):E * (t % 2) + E],
                                             comb[:, tt, bass.ds(col, 1)], xs[:, tt, :], ALU.mult, ALU.add).then_inc(added, 1)

            def experts(f):
                for e in range(8):
                    hidden(f, 0, e)
                    if e:
                        add(f, 0, e - 1)
                    route(f, e)
                last = UNITS // 2 - 1
                with dve.Fori(1, last) as i:
                    for e in range(8):
                        hidden(f, i, e)
                        if e:
                            add(f, i, e - 1)
                        else:
                            add(f, i - 1, 7)
                for e in range(8):
                    hidden(f, last, e)
                    add(f, last if e else last - 1, (e - 1) % 8)
                    if f == 0 and e in STATS_AT:
                        stats(2, STATS_AT.index(e))
                if f == 0:
                    normalise(2, 0)
                add(f, UNITS // 2 - 1, 7)

            for l in range(2):
                qkv(l)
                attention(l)
                between(l)
                experts(l)


def parts_of(a):
    found = []
    for _ in range(3):
        bits = a.astype(np.float32).view(np.uint32) & 0xFFFF0000
        found.append((bits >> 16).astype(np.uint16))
        a = a - bits.view(np.float32)
    return found


def shape_constants():
    p = np.arange(P)
    c = np.zeros((P, 3, P), np.float32)
    c[p, 0, p] = 1
    c[:, 1, :] = np.where(p[None, :] > p[:, None], NEG, 0)
    c[:, 2, :] = np.where(p[:, None] > p[None, :], NEG, 0)
    slope = (0.5 ** (np.arange(1, H + 1, dtype=np.float32) * 8.0 / H)).astype(np.float32)
    s = np.stack(parts_of(4 * slope) * 2)
    slopes = np.ascontiguousarray(np.broadcast_to(s[:, :, None], (ALIBI, H, N)))
    n = np.arange(N, dtype=np.float32)
    high = parts_of(np.floor(n / 8) * 8)[0]
    low = parts_of(n % 8)[0]
    one = parts_of(np.ones(N, np.float32))[0]
    krows = np.stack([high] * 3 + [low] * 3 + [one] * 3)
    iota = np.ascontiguousarray(np.broadcast_to(np.arange(NEXP, dtype=np.float32), (P, NEXP)))
    return c, slopes, krows, iota


def kernel(**inputs):
    import concourse.bacc as bacc
    from concourse.bass_utils import run_bass_kernel_spmd

    def get(name):
        return np.asarray(inputs["L0_" + name])

    w_qkv, b_qkv = get("attn_a_w_qkv"), get("attn_a_b_qkv")

    def by_dim(w):
        return w.reshape(-1, H, D).transpose(0, 2, 1).reshape(w.shape)

    w_a = np.concatenate([w_qkv[:, E:], w_qkv[:, :P - 2 * D], by_dim(w_qkv[:, :E])], 1)
    b_a = np.concatenate([b_qkv[E:], b_qkv[:P - 2 * D], by_dim(b_qkv[:E])]).reshape(3, P).T

    def fc_rows(w):
        return w.reshape(G // 2, 2, 4, D, E).transpose(2, 1, 3, 0, 4).reshape(P, G // 2, E)

    fc_a, fc_b = fc_rows(get("attn_a_w_fc")), fc_rows(get("attn_b_Wo").T)
    w_b = np.concatenate([by_dim(get("attn_b_Wq").T), by_dim(get("attn_b_Wk").T), get("attn_b_Wv").T], 1)
    router = np.zeros((E, P), np.float32)
    router[:, :NEXP] = get("ffn_router_w").T

    def unit_weights(gate, upw, down):
        def rows(w):
            return w.T.reshape(KE, P, P).transpose(1, 0, 2).reshape(P, E)
        return np.concatenate([rows(gate), rows(upw), down.T], 1)

    sw1, sw2, sw3, w12, w3 = (get("ffn_" + n) for n in ("sw1", "sw2", "sw3", "w12", "w3"))
    units = [unit_weights(sw1[P * n:P * n + P], sw2[P * n:P * n + P], sw3[:, P * n:P * n + P]) for n in range(8)]
    units += [unit_weights(w12[n, :P], w12[n, P:], w3[n]) for n in range(NEXP)]
    consts, slopes, krows, iota = shape_constants()
    arrays = {
        "x": get("attn_a_x"), "w_a": w_a, "b_a": b_a, "fc_a": fc_a, "b_fc": get("attn_a_b_fc"), "w_b": w_b, "fc_b": fc_b,
        "w_units": np.stack(units), "router": router, "ebias": get("ffn_expert_bias"), "iota": iota,
        "consts": consts, "slopes": slopes, "krows": krows,
    }
    nc = bacc.Bacc("TRN2", target_bir_lowering=False, num_devices=1)
    arrays = {f"{k}_dram": np.ascontiguousarray(v) for k, v in arrays.items()}
    args = [nc.dram_tensor(k, v.shape, mybir.dt.from_np(v.dtype), kind="ExternalInput").ap() for k, v in arrays.items()]
    args.append(nc.dram_tensor("out_dram", (NB, N, E), F32, kind="ExternalOutput").ap())
    program(nc, *args)
    r = run_bass_kernel_spmd(nc, [arrays], core_ids=[0])
    return r.results[0]["out_dram"]
```
